# Optimizing a Trainium2 kernel written in Bass

```python
import numpy as np
import jax
import jax.numpy as jnp

def _softmax(x, axis=-1):
    return jax.nn.softmax(x, axis=axis)

def _gelu(x):
    return jax.nn.gelu(x, approximate=True)

def _silu(x):
    return jax.nn.silu(x)

def _sigmoid(x):
    return jax.nn.sigmoid(x)

def _layernorm(x, axis=-1, eps=1e-05):
    m = jnp.mean(x, axis=axis, keepdims=True)
    v = jnp.var(x, axis=axis, keepdims=True)
    return (x - m) / jnp.sqrt(v + eps)

def _scatter_add(tgt, idx, src, axis=0):
    return tgt.at[idx].add(src)

def _segment_sum(src, seg, n):
    return jax.ops.segment_sum(src, seg, n)
kernel_name = 'mk_flamingo_gated_d1_seqx_r4_b26ce0'

def setup_inputs(seed: int=0):
    np.random.seed(seed)
    _w = jnp.asarray

    def _rec_inputs():
        import jax
        import jax.numpy as jnp
        _rk = jax.random.key(seed)
        x = -0.0003929 + 0.9999 * jax.random.normal(jax.random.fold_in(_rk, 1), (32, 256, 256), jnp.float32)
        _lenS = 256 - jax.random.randint(jax.random.fold_in(_rk, 7), (32,), 0, max(1, 256 // 4) + 1, jnp.int32)
        _lenS2 = 77 - jax.random.randint(jax.random.fold_in(_rk, 8), (32,), 0, max(1, 77 // 4) + 1, jnp.int32)
        _ctx_512P = jax.random.normal(jax.random.fold_in(_rk, 11), (32, 16, 128), jnp.float32)
        _ctx_512c = jax.random.dirichlet(jax.random.fold_in(_rk, 511), 0.3 * jnp.ones((16,), jnp.float32), (32, 77))
        _ctx_512t = jnp.einsum('bsk,bkd->bsd', _ctx_512c, _ctx_512P)
        _ctx_512t = _ctx_512t * jax.lax.rsqrt(jnp.mean(jnp.square(_ctx_512t)) + 1e-12) * 0.953939
        ctx_512 = -1.39393e-06 + 0.999914 * (_ctx_512t + 0.3 * jax.random.normal(jax.random.fold_in(_rk, 611), (32, 77, 128), jnp.float32))
        _g = jax.random.normal(jax.random.fold_in(_rk, 9001), (2, 1), jnp.float32)
        _g = jnp.sign(_g) * jnp.maximum(jnp.abs(_g), 1.0) + (_g == 0) * 1.0
        g_xattn = _g[0]
        g_ffn = _g[1]
        return (x, ctx_512, g_xattn, g_ffn)
    x, ctx_512, g_xattn, g_ffn = _rec_inputs()

    def _L0_xattn_setup():
        import jax, jax.numpy as jnp
        import numpy as np
        HEADS = 16
        D_MODEL = 256
        IMG_MODEL = 128
        D_K = D_MODEL // HEADS
        key = jax.random.key(seed)
        ks = jax.random.split(key, 12)
        B, LQ, LKV = (8, 512, 256)
        s_dm = 1.0 / np.sqrt(D_MODEL)
        s_im = 1.0 / np.sqrt(IMG_MODEL)
        return {'q': jax.random.normal(ks[0], (B, LQ, D_MODEL), jnp.float32), 'k': jax.random.normal(ks[1], (B, LKV, IMG_MODEL), jnp.float32), 'v': jax.random.normal(ks[2], (B, LKV, IMG_MODEL), jnp.float32), 'Wq': jax.random.normal(ks[3], (D_MODEL, D_MODEL), jnp.float32) * s_dm, 'bq': jnp.zeros((D_MODEL,), jnp.float32), 'Wk': jax.random.normal(ks[4], (IMG_MODEL, D_MODEL), jnp.float32) * s_im, 'bk': jnp.zeros((D_MODEL,), jnp.float32), 'Wv': jax.random.normal(ks[5], (IMG_MODEL, D_MODEL), jnp.float32) * s_im, 'bv': jnp.zeros((D_MODEL,), jnp.float32), 'Wo': jax.random.normal(ks[6], (D_MODEL, D_MODEL), jnp.float32) * s_dm, 'bo': jnp.zeros((D_MODEL,), jnp.float32)}
    _L0_xattn_all = _L0_xattn_setup()
    _L0_xattn_in = {k: v for k, v in _L0_xattn_all.items() if k in ('Wq', 'bq', 'Wk', 'bk', 'Wv', 'bv', 'Wo', 'bo')}
    del _L0_xattn_all

    def _L0_ffn_setup():
        import jax, jax.numpy as jnp
        import numpy as np
        TOP_K = 2
        NUM_EXPERTS = 8
        key = jax.random.key(seed)
        ks = jax.random.split(key, 8)
        h, d, ds, E = (256, 128, 256, NUM_EXPERTS)
        s = 1.0 / np.sqrt(h)
        return {'x': jax.random.normal(ks[0], (2, 512, h), jnp.float32), 'router': jax.random.normal(ks[1], (h, E), jnp.float32) * s, 'experts_gate': jax.random.normal(ks[2], (E, h, d), jnp.float32) * s, 'experts_up': jax.random.normal(ks[3], (E, h, d), jnp.float32) * s, 'experts_down': jax.random.normal(ks[4], (E, d, h), jnp.float32) * (1.0 / np.sqrt(d)), 'shared_gate': jax.random.normal(ks[5], (h, ds), jnp.float32) * s, 'shared_up': jax.random.normal(ks[6], (h, ds), jnp.float32) * s, 'shared_down': jax.random.normal(ks[7], (ds, h), jnp.float32) * (1.0 / np.sqrt(ds))}
    _L0_ffn_all = _L0_ffn_setup()
    _L0_ffn_in = {k: v for k, v in _L0_ffn_all.items() if k in ('router', 'experts_gate', 'experts_up', 'experts_down', 'shared_gate', 'shared_up', 'shared_down')}
    del _L0_ffn_all
    return {'x': x, 'ctx_512': ctx_512, 'g_xattn': g_xattn, 'g_ffn': g_ffn, 'L0_xattn_Wq': _L0_xattn_in['Wq'], 'L0_xattn_bq': _L0_xattn_in['bq'], 'L0_xattn_Wk': _L0_xattn_in['Wk'], 'L0_xattn_bk': _L0_xattn_in['bk'], 'L0_xattn_Wv': _L0_xattn_in['Wv'], 'L0_xattn_bv': _L0_xattn_in['bv'], 'L0_xattn_Wo': _L0_xattn_in['Wo'], 'L0_xattn_bo': _L0_xattn_in['bo'], 'L0_ffn_router': _L0_ffn_in['router'], 'L0_ffn_experts_gate': _L0_ffn_in['experts_gate'], 'L0_ffn_experts_up': _L0_ffn_in['experts_up'], 'L0_ffn_experts_down': _L0_ffn_in['experts_down'], 'L0_ffn_shared_gate': _L0_ffn_in['shared_gate'], 'L0_ffn_shared_up': _L0_ffn_in['shared_up'], 'L0_ffn_shared_down': _L0_ffn_in['shared_down']}

def reference(x, ctx_512, g_xattn, g_ffn, L0_xattn_Wq, L0_xattn_bq, L0_xattn_Wk, L0_xattn_bk, L0_xattn_Wv, L0_xattn_bv, L0_xattn_Wo, L0_xattn_bo, L0_ffn_router, L0_ffn_experts_gate, L0_ffn_experts_up, L0_ffn_experts_down, L0_ffn_shared_gate, L0_ffn_shared_up, L0_ffn_shared_down):
    import jax
    import jax.numpy as jnp

    def _L0_xattn_ref(q, k, v, Wq, bq, Wk, bk, Wv, bv, Wo, bo):
        import jax, jax.numpy as jnp
        import numpy as np
        HEADS = 16
        D_MODEL = 256
        IMG_MODEL = 128
        D_K = D_MODEL // HEADS
        B, LQ, _ = q.shape
        LKV = k.shape[1]
        qh = (q @ Wq + bq).reshape(B, LQ, HEADS, D_K).transpose(0, 2, 1, 3)
        kh = (k @ Wk + bk).reshape(B, LKV, HEADS, D_K).transpose(0, 2, 1, 3)
        vh = (v @ Wv + bv).reshape(B, LKV, HEADS, D_K).transpose(0, 2, 1, 3)
        scale = 1.0 / np.sqrt(D_K)
        scores = jnp.einsum('bhqd,bhkd->bhqk', qh, kh) * scale
        attn = jax.nn.softmax(scores, axis=-1)
        out = jnp.einsum('bhqk,bhkd->bhqd', attn, vh)
        concat = out.transpose(0, 2, 1, 3).reshape(B, LQ, D_MODEL)
        return concat @ Wo + bo

    def _L0_ffn_ref(x, router, experts_gate, experts_up, experts_down, shared_gate, shared_up, shared_down):
        import jax, jax.numpy as jnp
        import numpy as np
        TOP_K = 2
        NUM_EXPERTS = 8
        b, s, h = x.shape
        E = router.shape[1]
        shared_act = jax.nn.silu(jnp.einsum('bsh,hd->bsd', x, shared_gate))
        shared_up_out = jnp.einsum('bsh,hd->bsd', x, shared_up)
        shared_out = jnp.einsum('bsd,dh->bsh', shared_act * shared_up_out, shared_down)
        router_probs = jax.nn.softmax(jnp.einsum('bsh,he->bse', x, router), axis=-1)
        topk_probs, topk_idx = jax.lax.top_k(router_probs, TOP_K)
        coef = jnp.sum(jax.nn.one_hot(topk_idx, E, dtype=x.dtype) * topk_probs[..., None], axis=2)
        coef = coef.reshape(b * s, E)
        x_flat = x.reshape(b * s, h)
        gate = jnp.einsum('th,ehd->etd', x_flat, experts_gate)
        up = jnp.einsum('th,ehd->etd', x_flat, experts_up)
        expert_out = jnp.einsum('etd,edh->eth', jax.nn.silu(gate) * up, experts_down)
        routed = jnp.einsum('eth,te->th', expert_out, coef)
        return routed.reshape(b, s, h) + shared_out
    x = x + jnp.tanh(g_xattn[0]) * _L0_xattn_ref(_layernorm(x, axis=-1), ctx_512, ctx_512, L0_xattn_Wq, L0_xattn_bq, L0_xattn_Wk, L0_xattn_bk, L0_xattn_Wv, L0_xattn_bv, L0_xattn_Wo, L0_xattn_bo)
    x = x + jnp.tanh(g_ffn[0]) * _L0_ffn_ref(_layernorm(x, axis=-1), L0_ffn_router, L0_ffn_experts_gate, L0_ffn_experts_up, L0_ffn_experts_down, L0_ffn_shared_gate, L0_ffn_shared_up, L0_ffn_shared_down)
    return x

_drawn_inputs = setup_inputs


def setup_inputs(seed=0):
    import zlib

    import numpy as np

    out = dict(_drawn_inputs(seed))
    spreads = {'L0_xattn_bq': (0.0, 0.312),
     'L0_xattn_bk': (0.0, 0.8),
     'L0_xattn_bv': (0.0, 0.1),
     'L0_xattn_bo': (0.0, 0.1)}
    factors = {}
    for name, (base, spread) in spreads.items():
        noise = np.random.default_rng([zlib.crc32(name.encode()), seed]).standard_normal(out[name].shape)
        drawn = base * np.exp(spread * noise) if base else spread * noise
        out[name] = jnp.asarray(drawn.astype(out[name].dtype))
    for name, factor in factors.items():
        out[name] = (out[name] * factor).astype(out[name].dtype)
    return out
```

```python
from contextlib import ExitStack

import concourse.bass as bass
from concourse import mybir

F32 = mybir.dt.float32
F32R = mybir.dt.float32r
U32 = mybir.dt.uint32
ALU = mybir.AluOpType
ACT = mybir.ActivationFunctionType
AX = mybir.AxisListType

P = 128
B, S, D = 32, 256, 256
LK, DC = 77, 128
HEADS, DK = 16, 16
NG, HPG = 4, 4
GW = HPG * LK
LE = LK + LK % 2
NB = -(-GW // P)
REST = GW - (NB - 1) * P
TPB = S // P
KD = D // P
E, DE, DS = 8, 128, 256
NCH = DS // P + E
NSH = DS // P
FW = NCH * P
PAIR = 2 * S
TPP = PAIR // P
NPAIR = B * S // PAIR
EPS = 1e-5
PEEL = 5
N_SMALL = 10
SCALE = DK ** -0.5


class Step:

    def __init__(self, k, off):
        self.k, self.off = k, off

    @property
    def index(self):
        return self.k * 2 + self.off

    @property
    def parity(self):
        return self.off % 2

    def plus(self, n):
        return Step(self.k, self.off + n)

    def count(self, per, n):
        return self.k * (2 * per) + (per * self.off + n)


def reach(eng, sem, step, per, n):
    if isinstance(step.k, int):
        if step.count(per, n) > 0:
            eng.wait_ge(sem, step.count(per, n))
    else:
        assert per * step.off + n > 0, "a register may hold zero"
        eng.wait_ge(sem, step.count(per, n))


def landed(eng, sems, step, n=1):
    value = step.k * (16 * n) + (step.off // 2 + 1) * (16 * n)
    if isinstance(step.k, int):
        if value > 0:
            eng.wait_ge(sems[step.parity], value)
    else:
        assert step.off // 2 + 1 > 0, "a register may hold zero"
        eng.wait_ge(sems[step.parity], value)


def f32(ap):
    return ap.bitcast(F32)


def build(nc, x, ctx_in, g_xattn, g_ffn, Wq, bq, Wk, bk, Wv, bv, Wo, bo, router,
          e_gate, e_up, e_down, s_gate, s_up, s_down, ident_in, mask_in, iota_in, out):
    with ExitStack() as ctx:
        def sb(name, shape, dt=F32):
            return ctx.enter_context(nc.sbuf_tensor(name, shape, dt))

        def sem(name):
            return ctx.enter_context(nc.semaphore(name))

        ident = sb("ident", [P, P])
        mask = sb("mask", [P, 2, HPG])
        iota = sb("iota", [P, E])
        gains = sb("gains", [P, 4])
        bq_c = sb("bq_c", [P, KD])
        bk_c = sb("bk_c", [P, NG])
        bv_c = sb("bv_c", [P, KD])
        bv_b = sb("bv_b", [P, 2, KD, P], F32R)
        bo_g = sb("bo_g", [P, D])
        half_neg = sb("half_neg", [P, TPP])
        eps = sb("eps", [P, TPP])
        gate = sb("gate", [P, 4])
        wq = sb("wq", [P, 2, KD, D], F32R)
        wk = sb("wk", [P, 2, NG, P], F32R)
        wv = sb("wv", [P, 2, D], F32R)
        wo = sb("wo", [P, 2, KD, D], F32R)
        wr = sb("wr", [P, 2, KD, P], F32R)
        wg = sb("wg", [P, 2, KD, FW], F32R)
        wu = sb("wu", [P, 2, KD, FW], F32R)
        wd = sb("wd", [P, 2, NCH, D], F32R)

        xin = sb("xin", [P, 2, TPB, D])
        cin = sb("cin", [LK, 2, DC])
        xres = sb("xres", [P, 2, TPB, D])
        xbias = sb("xbias", [P, TPB, D])
        x1b = sb("x1b", [P, 2, TPB, D])
        stats = sb("stats", [P, TPP, 6])
        mv = sb("mv", [P, TPP, 2])
        rstd = sb("rstd", [P, TPP])
        xh = sb("xh", [P, TPB, D])
        xT = sb("xT", [P, 2, KD, S], F32R)
        cT = sb("cT", [P, 2, 2, NB * P], F32R)
        qf = sb("qf", [P, KD, S])
        qst = sb("qst", [P, NG, S], F32R)
        kt = sb("kt", [P, NG, LK])
        kt2 = sb("kt2", [P, 2, NG, LK], F32R)
        kbd = sb("kbd", [P, 2, NG, LK, HPG], F32R)
        vm = sb("vm", [P, NB * NG, HPG, DK])
        vbd = sb("vbd", [P, NB * NG, 2, HPG * DK], F32R)
        pr = sb("pr", [P, 2, TPB, NG, GW])
        mx = sb("mx", [P, 2, HEADS // 2])
        den = sb("den", [P, TPB, HEADS])
        rden = sb("rden", [P, TPB, HEADS])
        pT = sb("pT", [P, 2, NB * NG, S], F32R)
        otmp = sb("otmp", [64, KD, 2 * S])
        of = sb("of", [P, KD, S])
        oT = sb("oT", [P, 2, KD, S], F32R)

        x2T = sb("x2T", [P, 2, 2, KD, PAIR], F32R)
        sil = [qf[:].rearrange("p a b -> p (a b)"), of[:].rearrange("p a b -> p (a b)")]

        taken = [0]

        def over_pr(*dims):
            n = 1
            for d in dims:
                n *= d
            taken[0] += n
            flat = pr[:].rearrange("p a t g n -> p (a t g n)")[:, taken[0] - n:taken[0]]
            names = "abc"[:len(dims)]
            return flat.rearrange(f"p ({' '.join(names)}) -> p {' '.join(names)}", **dict(zip(names, dims))) \
                if len(dims) > 1 else flat

        x1p = over_pr(2, TPP, D)
        xh2 = over_pr(TPP, D)
        hf = over_pr(2, PAIR)
        lgT = over_pr(PAIR)[0:E]
        lg = over_pr(TPP, E)
        top = over_pr(TPP, 8)
        topi = over_pr(TPP, 8).bitcast(U32)
        topf = over_pr(TPP, 8)
        ex = over_pr(TPP, E)
        hot = over_pr(2, TPP, E)
        esum = over_pr(TPP)
        einv = over_pr(TPP)
        coef = over_pr(2, TPP, E)
        h2 = pT[:].rearrange("p a b c -> p (a b c)")[:, 0:4 * PAIR].rearrange("p (a b c) -> p a b c", a=2, b=2)

        psS = ctx.enter_context(nc.psum_tensor("psS", [P, 4, 512], F32))
        psT = ctx.enter_context(nc.psum_tensor("psT", [P, 2, 512], F32))
        psM = ctx.enter_context(nc.psum_tensor("psM", [P, 2, 512], F32))
        x1_dram = nc.dram_tensor("x1_scratch", (B * S, D), F32, kind="Internal").ap()

        (w_in, w_hi, w_lo, w_zero, w_gain, w_bias, w_bvwo) = map(sem, (
            "w_in", "w_hi", "w_lo", "w_zero", "w_gain", "w_bias", "w_bvwo"))
        w_stage = [sem("w_stage0"), sem("w_stage1")]
        a_x = [sem("a_in0"), sem("a_in1")]
        a_res = [sem("a_res0"), sem("a_res1")]
        a_st = [sem("a_st0"), sem("a_st1")]
        (a_stat, a_mv, a_eps, a_rstd, a_xh, a_xTp, a_xThi, a_xTlo, a_cTp, a_cThi, a_cTlo, a_q, a_qf, a_qhi,
         a_qlo, a_k, a_kt, a_kthi, a_ktlo, a_kbhi, a_kblo, a_s, a_mx, a_sub, a_exp, a_den, a_rden, a_pn,
         a_pTp, a_pThi, a_pTlo, a_o, a_otmp, a_of, a_ohi, a_olo, a_v, a_vm, a_vhi, a_vlo, a_wo,
         a_xb, a_x1) = [sem("a_" + n) for n in (
            "stat mv eps rstd xh xTp xThi xTlo cTp cThi cTlo q qf qhi qlo k kt kthi ktlo kbhi kblo s mx "
            "sub exp den rden pn pTp pThi pTlo o otmp of ohi olo v vm vhi vlo wo xb x1").split()]
        b_x = [sem("b_x0"), sem("b_x1")]
        b_st = [sem("b_st0"), sem("b_st1")]
        (b_stat, b_mv, b_eps, b_rstd, b_xh, b_xTp, b_xThi, b_xTlo, b_lgp, b_lgT, b_lgt, b_lg, b_top, b_topi,
         b_topf, b_sub, b_exp, b_sum, b_inv, b_hot, b_sel, b_cf, b_g, b_u, b_sil, b_h, b_hhi, b_hlo, b_y,
         b_acc) = [sem("b_" + n) for n in (
            "stat mv eps rstd xh xTp xThi xTlo lgp lgT lgt lg top topi topf sub exp sum inv hot sel cf "
            "g u sil h hhi hlo y acc").split()]

        block = ctx.enter_context(nc.Block())

        stage = [pr[:, i].rearrange("p t g n -> p (t g n)") for i in range(2)]
        rows = lambda w: w.rearrange("(k p) n -> p k n", p=P)
        one = lambda t, i: t[:, i].rearrange("p a b -> p (a b)") if len(t.shape) == 4 else t[:, i]
        jobs = [([(rows(Wq), 0, (KD, D))], lambda i: one(wq, i), KD * D),
                ([(Wk.rearrange("p (g n) -> p g n", g=NG), 64 * r, (NG, P, 64)) for r in range(2)],
                 lambda i: one(wk, i), NG * P),
                ([(Wv, 0, None)], lambda i: wv[:, i], D),
                ([(rows(Wo), 0, (KD, D))], lambda i: one(wo, i), KD * D),
                ([(rows(router), 0, (KD, E))], lambda i: wr[:, i, :, 0:E], KD * E)]
        for w_s, w_e, target in ((s_gate, e_gate, wg), (s_up, e_up, wu)):
            for k in range(KD):
                jobs.append(([(w_s[k * P:(k + 1) * P, :], 0, None),
                              (w_e[:, k * P:(k + 1) * P, :].rearrange("e p d -> p e d"), DS, (E, DE))],
                             lambda i, k=k, target=target: target[:, i, k, :], FW))
        for h in range(2):
            n0, n1 = (0, 5) if h == 0 else (5, NCH)
            parts = ([(rows(s_down), 0, (NSH, D))] if h == 0 else [])
            m0 = NSH if h == 0 else n0
            parts.append((e_down[m0 - NSH:n1 - NSH].rearrange("e p d -> p e d"), (m0 - n0) * D, (n1 - m0, D)))
            jobs.append((parts, lambda i, n0=n0, n1=n1: wd[:, i, n0:n1, :].rearrange("p a b -> p (a b)"),
                         (n1 - n0) * D))

        def staged(n):
            parts, target, width = jobs[n]
            v = stage[n % 2][:, 0:width]
            return v.rearrange("p (a b) -> p a b", a=KD) if n == 4 else v

        job_parts = [sum(len(j[0]) for j in jobs[n % 2:n + 1:2]) for n in range(len(jobs))]

        @block.sync
        def _(sp):
            def load_x(b):
                reach(sp, a_xh, b, 1, -1)
                reach(sp, a_cTp, b, 1, -1)
                sp.dma_start(xin[:, b.parity], x[b.index].rearrange("(t p) d -> p t d", p=P)
                             ).then_inc(a_x[b.parity], 16)
                sp.dma_start(cin[:, b.parity], ctx_in[b.index]).then_inc(a_x[b.parity], 16)

            def load_res(b):
                reach(sp, a_xb, b, 1, -1)
                sp.dma_start(xres[:, b.parity], x[b.index].rearrange("(t p) d -> p t d", p=P)
                             ).then_inc(a_res[b.parity], 16)

            def store_x1(b):
                reach(sp, a_x1, b, 1, 1)
                sp.dma_start(x1_dram[bass.ds(b.index * S, S), :].rearrange("(t p) d -> p t d", p=P),
                             x1b[:, b.parity]).then_inc(a_st[b.parity], 16)

            def load_x1(p):
                landed(sp, b_st, p.plus(-2))
                sp.dma_start(x1p[:, p.parity],
                             x1_dram[bass.ds(p.index * PAIR, PAIR), :].rearrange("(t p) d -> p t d", p=P)
                             ).then_inc(b_x[p.parity], 16)

            def store_out(p):
                reach(sp, b_acc, p, NCH - NSH + 1, NCH - NSH + 1)
                sp.dma_start(out[bass.ds(p.index * PAIR, PAIR), :].rearrange("(t p) d -> p t d", p=P),
                             x1p[:, p.parity]).then_inc(b_st[p.parity], 16)

            load_x(Step(0, 0))
            small = [(ident[:], ident_in), (mask[:], mask_in), (iota[:], iota_in),
                     (gains[:, 0:1], g_xattn.rearrange("(a b) -> a b", a=1).partition_broadcast(P)),
                     (gains[:, 1:2], g_ffn.rearrange("(a b) -> a b", a=1).partition_broadcast(P)),
                     (bq_c[:], bq.rearrange("(m p) -> p m", p=P)),
                     (bk_c[0:64, :], bk.rearrange("(g p) -> p g", p=64)),
                     (bk_c[64:P, :], bk.rearrange("(g p) -> p g", p=64)),
                     (bv_c[:], bv.rearrange("(m p) -> p m", p=P)),
                     (bo_g[:], bo.rearrange("(a b) -> a b", a=1).partition_broadcast(P))]
            for dst, src in small:
                sp.dma_start(dst, src, allow_slow_non_contiguous=True).then_inc(w_in, 16)
            for n, (parts, target, width) in enumerate(jobs):
                if n >= 2:
                    sp.wait_ge(w_lo, n - 1)
                for src, at, dims in parts:
                    dst = stage[n % 2]
                    if dims is None:
                        dst = dst[:, at:at + src.shape[1]]
                    elif len(dims) == 2:
                        dst = dst[:, at:at + dims[0] * dims[1]].rearrange("p (a b) -> p a b", a=dims[0])
                    else:
                        dst = dst[:, 0:dims[0] * dims[1]].rearrange("p (a b) -> p a b", a=dims[0])[
                            :, :, at:at + dims[2]]
                    sp.dma_start(dst, src).then_inc(w_stage[n % 2], 16)
            load_x(Step(0, 1))

            def iteration(i):
                last = isinstance(i.k, int)
                if not last or i.off + 2 < B:
                    load_x(i.plus(2))
                if not last or 1 <= i.off <= B:
                    load_res(i.plus(-1))
                if not last or i.off >= 2:
                    store_x1(i.plus(-2))

            for i in range(PEEL):
                iteration(Step(0, i))
            with sp.Fori(0, (B - 3 - PEEL) // 2) as k:
                iteration(Step(k, PEEL))
                iteration(Step(k, PEEL + 1))
            for i in range(B - 3, B + 2):
                iteration(Step(0, i))

            landed(sp, a_st, Step(0, B - 2))
            landed(sp, a_st, Step(0, B - 1))
            load_x1(Step(0, 0))
            load_x1(Step(0, 1))
            store_out(Step(0, 0))
            with sp.Fori(0, (NPAIR - 2) // 2) as k:
                for off in (1, 2):
                    load_x1(Step(k, off + 1))
                    store_out(Step(k, off))
            store_out(Step(0, NPAIR - 1))
            landed(sp, b_st, Step(0, NPAIR - 2))
            landed(sp, b_st, Step(0, NPAIR - 1))

        @block.tensor
        def _(pe):
            mm = nc.tensor.matmul

            def scores(i):
                for s in range(4):
                    t, hh = s // 2, s % 2
                    if s == 0:
                        reach(pe, a_qhi, i, 1, 1)
                        reach(pe, a_qlo, i, 2, 2)
                        reach(pe, a_kbhi, i, 1, 1)
                        reach(pe, a_kblo, i, 1, 1)
                    reach(pe, a_sub, i, 4, s - 1)
                    for g2 in range(2):
                        g = 2 * hh + g2
                        for part in range(2):
                            last = mm(psS[:, 2 * (s % 2) + g2, 0:GW], qst[:, g, t * P:(t + 1) * P],
                                      kbd[:, part, g].rearrange("p k j -> p (k j)"),
                                      start=(part == 0), stop=(part == 1))
                    last.then_inc(a_s, 1)

            def out_proj(i):
                reach(pe, a_ohi, i, 1, 1)
                reach(pe, a_olo, i, 1, 1)
                reach(pe, a_pTlo, i, 6, 6)
                for t in range(TPB):
                    n = 0
                    for m in range(KD):
                        for a, w in ((0, 0), (0, 1), (1, 0)):
                            last = mm(psT[:, 1, t * D:(t + 1) * D], oT[:, a, m, t * P:(t + 1) * P],
                                      wo[:, w, m, :], start=(n == 0), stop=(n == 5))
                            n += 1
                last.then_inc(a_wo, 1)

            def front(b):
                reach(pe, a_xh, b, 1, 1)
                reach(pe, a_otmp, b, 1, -2)
                reach(pe, a_of, b, 1, -2)
                for k in range(KD):
                    for t in range(TPB):
                        last = nc.tensor.transpose(psM[:, 0, k * S + t * P:k * S + (t + 1) * P],
                                                   xh[:, t, k * P:(k + 1) * P], ident[:])
                last.then_inc(a_xTp, 1)
                landed(pe, a_x, b, 2)
                nc.tensor.transpose(psM[:, 1, 0:LK], cin[:, b.parity], ident[0:LK, 0:LK]).then_inc(a_cTp, 1)
                reach(pe, a_xThi, b, 1, 1)
                reach(pe, a_xTlo, b, 1, 1)
                for m in range(KD):
                    n = 0
                    for k in range(KD):
                        for w, a in ((0, 0), (1, 0), (0, 1)):
                            last = mm(psM[:, 0, m * S:(m + 1) * S], wq[:, w, k, m * P:(m + 1) * P],
                                      xT[:, a, k, :], start=(n == 0), stop=(n == 5))
                            n += 1
                last.then_inc(a_q, 1)
                reach(pe, a_cThi, b, 1, 1)
                reach(pe, a_cTlo, b, 1, 1)
                for g in range(NG):
                    for n, (w, a) in enumerate(((0, 0), (1, 0), (0, 1))):
                        last = mm(psM[:, 1, g * LE:(g + 1) * LE], wk[:, w, g, :], cT[:, b.parity, a, 0:LE * HPG:HPG],
                                  start=(n == 0), stop=(n == 2))
                last.then_inc(a_k, 1)

            def values(b):
                reach(pe, a_cThi, b, 1, 1)
                reach(pe, a_cTlo, b, 1, 1)
                reach(pe, a_pTlo, b.plus(-1), 6, 6)
                for blk in range(NB):
                    for n, (a, w) in enumerate(((0, 0), (0, 1), (1, 0))):
                        last = mm(psT[:, blk // 2, (blk % 2) * D:(blk % 2 + 1) * D],
                                  cT[:, b.parity, a, blk * P:(blk + 1) * P], wv[:, w, :], start=(n == 0), stop=(n == 2))
                last.then_inc(a_v, 1)

            def attend(b):
                for s in range(2 * NB):
                    t, blk = s // NB, s % NB
                    rows_of = P if blk < NB - 1 else REST
                    if blk == 0:
                        reach(pe, a_pn, b, 2, t + 1)
                    if s == 0:
                        reach(pe, a_vm, b, 1, 1)
                    if s == 1:
                        reach(pe, a_x1, b, 1, 0)
                    if s >= 2 and blk < NB - 1:
                        reach(pe, a_pTlo, b, 6, s - 1)
                    for g in range(NG):
                        if blk == NB - 2 and g == NG - 1:
                            reach(pe, a_pTlo, b, 6, s)
                        last = nc.tensor.transpose(psT[0:rows_of, s % 2, g * P:(g + 1) * P],
                                                   pr[:, b.parity, t, g, blk * P:blk * P + rows_of], ident[:])
                    last.then_inc(a_pTp, 1)
                reach(pe, a_pThi, b, 6, 6)
                reach(pe, a_pTlo, b, 6, 6)
                reach(pe, a_vhi, b, 1, 1)
                reach(pe, a_vlo, b, 1, 1)
                for g in range(NG):
                    n = 0
                    for blk in range(NB):
                        rows_of = P if blk < NB - 1 else REST
                        for part in range(2):
                            last = mm(psM[:, g // 2, (g % 2) * S:(g % 2 + 1) * S],
                                      vbd[0:rows_of, blk * NG + g].rearrange("p a b -> p (a b)"),
                                      pT[0:rows_of, part, blk * NG + g, :], start=(n == 0), stop=(n == 2 * NB - 1))
                            n += 1
                last.then_inc(a_o, 1)

            def iteration(i):
                last = isinstance(i.k, int)
                if not last or i.off < B:
                    scores(i)
                if not last or i.off >= 2:
                    out_proj(i.plus(-2))
                if not last or i.off + 1 < B:
                    front(i.plus(1))
                if not last or 1 <= i.off <= B:
                    nxt = i.plus(1) if (not last or i.off + 1 < B) else Step(0, B - 1)
                    reach(pe, a_qf, nxt, 1, 1)
                    reach(pe, a_kt, nxt, 1, 1)
                    attend(i.plus(-1))
                if not last or i.off < B:
                    values(i)

            pe.wait_ge(w_lo, 2)
            pe.wait_ge(w_hi, 2)
            pe.wait_ge(w_in, 16 * N_SMALL)
            pe.wait_ge(w_lo, len(jobs))
            pe.wait_ge(w_bias, 2)
            n = 0
            for m in range(KD):
                for a, w in ((0, 0), (0, 1), (1, 0)):
                    last = mm(psT[:, 0, 0:D], bv_b[:, a, m, :], wo[:, w, m, :], start=(n == 0), stop=(n == 5))
                    n += 1
            last.then_inc(w_bvwo, 1)
            front(Step(0, 0))
            for i in range(PEEL):
                iteration(Step(0, i))
            with pe.Fori(0, (B - 1 - PEEL) // 2) as k:
                iteration(Step(k, PEEL))
                iteration(Step(k, PEEL + 1))
            for i in range(B - 1, B + 2):
                iteration(Step(0, i))

            def transposes(p):
                reach(pe, b_xh, p, 1, 1)
                reach(pe, b_lg, p, 1, 0)
                for k in range(KD):
                    for t in range(TPP):
                        last = nc.tensor.transpose(psM[:, k, t * P:(t + 1) * P],
                                                   xh2[:, t, k * P:(k + 1) * P], ident[:])
                    last.then_inc(b_xTp, 1)

            def route(p):
                reach(pe, b_xThi, p, 2, 2)
                reach(pe, b_xTlo, p, 2, 2)
                n = 0
                for k in range(KD):
                    for w, a in ((0, 0), (1, 0), (0, 1)):
                        last = mm(psM[:, 0, :], wr[:, w, k, :], x2T[:, p.parity, a, k, :],
                                  start=(n == 0), stop=(n == 5))
                        n += 1
                last.then_inc(b_lgp, 1)

            def route_back(p):
                if isinstance(p.k, int):
                    reach(pe, b_lgT, p, 1, 1)
                for t in range(TPP):
                    last = nc.tensor.transpose(psM[:, 1, t * E:(t + 1) * E], lgT[:, t * P:(t + 1) * P],
                                               ident[0:E, 0:E])
                last.then_inc(b_lgt, 1)

            def gate_up(p, m):
                c = m % 2
                reach(pe, b_h, p, NCH, m - 1)
                for w2, base, done in ((wg, 0, b_g), (wu, 1, b_u)):
                    n = 0
                    for k in range(KD):
                        for w, a in ((0, 0), (1, 0), (0, 1)):
                            last = mm(psS[:, 2 * c + base, :], w2[:, w, k, m * P:(m + 1) * P],
                                      x2T[:, p.parity, a, k, :], start=(n == 0), stop=(n == 5))
                            n += 1
                    last.then_inc(done, 1)

            def down(p, m, ahead=False):
                c = m % 2
                reach(pe, b_hhi, p, NCH, m + 1)
                reach(pe, b_hlo, p, NCH, m + 1)
                if m != 1:
                    reach(pe, b_acc, p, NCH - NSH + 1, max(m - 1, 0))
                for t in range(TPP):
                    if ahead and t == TPP - 1:
                        reach(pe, b_lgT, p.plus(1), 1, 1)
                    for n, (a, w) in enumerate(((0, 0), (0, 1), (1, 0))):
                        if m < NSH:
                            start = m == 0 and n == 0 and t % 2 == 0
                            stop = m == NSH - 1 and n == 2
                        else:
                            start, stop = n == 0, n == 2
                        last = mm(psT[:, t // 2, (t % 2) * D:(t % 2 + 1) * D],
                                  h2[:, c, a, t * P:(t + 1) * P], wd[:, w, m, :],
                                  start=start, stop=stop, skip_group_check=(m < NSH))
                last.then_inc(b_y, 1)

            def pair(p, prep, nxt):
                for m in range(NCH):
                    if m + 1 < NCH:
                        gate_up(p, m + 1)
                    elif nxt:
                        gate_up(p.plus(1), 0)
                    down(p, m, prep and m == 5)
                    if prep and m == 3:
                        transposes(p.plus(1))
                    if prep and m == 4:
                        route(p.plus(1))
                    if prep and m == 5:
                        route_back(p.plus(1))

            transposes(Step(0, 0))
            route(Step(0, 0))
            route_back(Step(0, 0))
            gate_up(Step(0, 0), 0)
            pair(Step(0, 0), True, True)
            with pe.Fori(0, (NPAIR - 2) // 2) as k:
                pair(Step(k, 1), True, True)
                pair(Step(k, 2), True, True)
            pair(Step(0, NPAIR - 1), False, False)

        @block.scalar
        def _(act):
            act.wait_ge(w_in, 16 * N_SMALL)
            nc.scalar.activation(gains[:, 2:4], gains[:, 0:2], ACT.Tanh).then_inc(w_gain, 1)
            for n, (parts, target, width) in enumerate(jobs):
                act.wait_ge(w_stage[n % 2], 16 * job_parts[n])
                if n == 4:
                    act.wait_ge(w_zero, 1)
                nc.scalar.copy(target(0), staged(n)).then_inc(w_hi, 1)

            def front_x(b):
                reach(act, a_xTp, b, 1, 1)
                reach(act, a_q, b, 1, 0)
                nc.scalar.copy(xT[:, 0].rearrange("p a b -> p (a b)"), psM[:, 0, :]).then_inc(a_xThi, 1)
                reach(act, a_cTp, b, 1, 1)
                reach(act, a_v, b, 1, -1)
                nc.scalar.copy(cT[:, b.parity, 0, 0:GW].rearrange("p (k j) -> p k j", j=HPG),
                               psM[:, 1, 0:LK].unsqueeze(2).broadcast_to([P, LK, HPG])).then_inc(a_cThi, 1)

            def front_q(b):
                reach(act, a_q, b, 1, 1)
                reach(act, a_qlo, b, 2, 0)
                for m in range(KD):
                    last = nc.scalar.activation(qf[:, m, :], psM[:, 0, m * S:(m + 1) * S], ACT.Identity,
                                                bias=bq_c[:, m:m + 1])
                last.then_inc(a_qf, 1)
                reach(act, a_s, b, 4, 0)
                reach(act, a_qf, b, 1, 1)
                for r in range(2):
                    rs = slice(64 * r, 64 * r + 64)
                    last = nc.scalar.copy(qst[rs, r::2, :], qf[rs, :, :])
                last.then_inc(a_qhi, 1)
                reach(act, a_kt, b, 1, 1)
                reach(act, a_kbhi, b, 1, 0)
                nc.scalar.copy(kt2[:, 0], kt[:]).then_inc(a_kthi, 1)
                reach(act, a_ktlo, b, 1, 1)
                for j in range(HPG):
                    last = nc.scalar.activation(kbd[:, 1, :, :, j], f32(kt2[:, 1]), ACT.Copy,
                                                scale=mask[:, 0, j:j + 1])
                last.then_inc(a_kblo, 1)

            def exps(i, s):
                t, hh = s // 2, s % 2
                reach(act, a_sub, i, 4, s + 1)
                v = pr[:, i.parity, t, 2 * hh:2 * hh + 2, :]
                nc.scalar.activation(v, v, ACT.Exp, scale=SCALE).then_inc(a_exp, 1)

            def attend(b):
                for s in range(2 * NB):
                    t, blk = s // NB, s % NB
                    rs = slice(0, P if blk < NB - 1 else REST)
                    reach(act, a_pTp, b, 6, s + 1)
                    if s == 0:
                        reach(act, a_o, b, 1, 0)
                    nc.scalar.copy(pT[rs, 0, NG * blk:NG * (blk + 1), t * P:(t + 1) * P],
                                   psT[rs, s % 2, :].rearrange("p (g n) -> p g n", g=NG)).then_inc(a_pThi, 1)
                reach(act, a_o, b, 1, 1)
                reach(act, a_of, b, 1, 0)
                nc.scalar.copy(otmp[:], psM[64:P, :, :]).then_inc(a_otmp, 1)

            def attend_hi(b):
                reach(act, a_of, b, 1, 1)
                reach(act, a_wo, b, 1, 0)
                nc.scalar.copy(oT[:, 0], of[:]).then_inc(a_ohi, 1)

            def values(b):
                reach(act, a_vm, b, 1, 1)
                reach(act, a_o, b, 1, 0)
                nc.scalar.copy(vbd[:, :, 0, :], vm[:].rearrange("p a j d -> p a (j d)")).then_inc(a_vhi, 1)

            def iteration(i):
                last = isinstance(i.k, int)
                if not last or i.off < B:
                    for s in range(4):
                        exps(i, s)
                if not last or i.off + 1 < B:
                    front_x(i.plus(1))
                    front_q(i.plus(1))
                if not last or 1 <= i.off <= B:
                    attend(i.plus(-1))
                if not last or i.off < B:
                    values(i)
                if not last or 1 <= i.off <= B:
                    attend_hi(i.plus(-1))

            act.wait_ge(w_zero, 4)
            front_x(Step(0, 0))
            front_q(Step(0, 0))
            for i in range(PEEL):
                iteration(Step(0, i))
            with act.Fori(0, (B - 1 - PEEL) // 2) as k:
                iteration(Step(k, PEEL))
                iteration(Step(k, PEEL + 1))
            for i in range(B - 1, B + 2):
                iteration(Step(0, i))

            def hi(p):
                for k in range(KD):
                    reach(act, b_xTp, p, 2, k + 1)
                    nc.scalar.copy(x2T[:, p.parity, 0, k, :], psM[:, k, :]).then_inc(b_xThi, 1)

            def logits(p):
                reach(act, b_lgp, p, 1, 1)
                reach(act, b_lgt, p, 1, 0)
                nc.scalar.copy(lgT[:], psM[0:E, 0, :]).then_inc(b_lgT, 1)

            def exp(p):
                reach(act, b_sub, p, 1, 1)
                nc.scalar.activation(ex[:], ex[:], ACT.Exp).then_inc(b_exp, 1)

            def chunk(p, m):
                reach(act, b_g, p, NCH, m + 1)
                reach(act, b_h, p, NCH, m - 1)
                nc.scalar.activation(sil[m % 2], psS[:, 2 * (m % 2), :], ACT.Silu).then_inc(b_sil, 1)
                reach(act, b_h, p, NCH, m + 1)
                reach(act, b_y, p, NCH, m - 1)
                nc.scalar.copy(h2[:, m % 2, 0, :], hf[:, m % 2, :]).then_inc(b_hhi, 1)

            def pair(p, prep):
                for m in range(NCH):
                    chunk(p, m)
                    if prep and m == 4:
                        hi(p.plus(1))
                    if prep and m == 5:
                        logits(p.plus(1))
                    if prep and m == 7:
                        exp(p.plus(1))

            hi(Step(0, 0))
            logits(Step(0, 0))
            exp(Step(0, 0))
            pair(Step(0, 0), True)
            with act.Fori(0, (NPAIR - 2) // 2) as k:
                pair(Step(k, 1), True)
                pair(Step(k, 2), True)
            pair(Step(0, NPAIR - 1), False)

        @block.vector
        def _(dve):
            V = nc.vector
            V.memset(f32(wr[:]), 0.0).then_inc(w_zero, 1)
            V.memset(eps[:], EPS).then_inc(w_zero, 1)
            V.memset(half_neg[:], -0.5).then_inc(w_zero, 1)
            V.memset(f32(cT[:]), 0.0).then_inc(w_zero, 1)
            dve.wait_ge(w_in, 16 * N_SMALL)
            bv_cols = bv_c[:].unsqueeze(2).broadcast_to([P, KD, P])
            V.tensor_copy(bv_b[:, 0], bv_cols).then_inc(w_bias, 1)
            dve.wait_ge(w_bias, 1)
            V.tensor_tensor(bv_b[:, 1], bv_cols, f32(bv_b[:, 0]), ALU.subtract).then_inc(w_bias, 1)

            def stats_of(b, src, done):
                for t in range(TPB):
                    V.bn_stats(stats[:, t, :], src[:, t, :]).then_inc(a_stat, 1)
                reach(dve, a_stat, b, TPB, TPB)
                V.memset(gate[:, 0:1], 0.0)
                for t in range(TPB):
                    last = V.bn_aggr(mv[:, t, :], stats[:, t, :])
                last.then_inc(done, 1)

            def norm_stats(b):
                landed(dve, a_x, b, 2)
                stats_of(b, xin[:, b.parity], a_mv)

            def norm(b):
                reach(dve, a_rstd, b, 1, 1)
                reach(dve, a_mv, b, 1, 1)
                reach(dve, a_xTp, b, 1, 0)
                for t in range(TPB):
                    last = V.tensor_scalar(xh[:, t, :], xin[:, b.parity, t, :], mv[:, t, 0:1], rstd[:, t:t + 1],
                                           ALU.subtract, ALU.mult)
                last.then_inc(a_xh, 1)

            def split_weights():
                for n, (parts, target, width) in enumerate(jobs):
                    dve.wait_ge(w_hi, n + 1)
                    V.tensor_tensor(target(1), staged(n), f32(target(0)), ALU.subtract
                                    ).then_inc(w_lo, 1)
                dve.wait_ge(w_lo, len(jobs))

            def shift(i, s):
                t, hh = s // 2, s % 2
                reach(dve, a_s, i, 4, s + 1)
                bank = psS[:, 2 * (s % 2):2 * (s % 2) + 2, 0:GW]
                reach(dve, a_sub, i, 4, s - 1)
                V.tensor_reduce(mx[:, s % 2, :], bank.rearrange("p g (k j) -> p g j k", j=HPG), AX.X, ALU.max
                                ).then_inc(a_mx, 1)
                reach(dve, a_mx, i, 4, s + 1)
                if s == 0:
                    reach(dve, a_pTp, i, 6, -6)
                V.tensor_tensor(
                    pr[:, i.parity, t, 2 * hh:2 * hh + 2, :].rearrange("p g (k j) -> p g k j", j=HPG),
                    bank.rearrange("p g (k j) -> p g k j", j=HPG),
                    mx[:, s % 2, :].rearrange("p (g j) -> p g j", g=2).unsqueeze(2).broadcast_to([P, 2, LK, HPG]),
                    ALU.subtract).then_inc(a_sub, 1)

            def sums(i, t):
                reach(dve, a_exp, i, 4, 2 * t + 2)
                reach(dve, a_rden, i, 2, t - 1)
                V.tensor_reduce(den[:, t, :], pr[:, i.parity, t].rearrange("p g (k j) -> p g j k", j=HPG),
                                AX.X, ALU.add).then_inc(a_den, 1)
                reach(dve, a_den, i, 2, t + 1)
                reach(dve, a_pn, i, 2, t - 1)
                V.reciprocal(rden[:, t, :], den[:, t, :]).then_inc(a_rden, 1)

            def residual(i):
                reach(dve, a_wo, i, 1, 1)
                reach(dve, a_xb, i, 1, 1)
                landed(dve, a_st, i.plus(-2))
                V.scalar_tensor_tensor(x1b[:, i.parity].rearrange("p a b -> p (a b)"), psT[:, 1, :],
                                       gains[:, 2:3], xbias[:].rearrange("p a b -> p (a b)"),
                                       ALU.mult, ALU.add).then_inc(a_x1, 1)

            def front(b):
                reach(dve, a_xThi, b, 1, 1)
                V.tensor_tensor(xT[:, 1].rearrange("p a b -> p (a b)"), psM[:, 0, :],
                                f32(xT[:, 0]).rearrange("p a b -> p (a b)"), ALU.subtract).then_inc(a_xTlo, 1)
                reach(dve, a_cThi, b, 1, 1)
                V.tensor_tensor(cT[:, b.parity, 1, 0:GW].rearrange("p (k j) -> p k j", j=HPG),
                                psM[:, 1, 0:LK].unsqueeze(2).broadcast_to([P, LK, HPG]),
                                f32(cT[:, b.parity, 0, 0:GW]).rearrange("p (k j) -> p k j", j=HPG), ALU.subtract
                                ).then_inc(a_cTlo, 1)
                reach(dve, a_k, b, 1, 1)
                reach(dve, a_kthi, b, 1, 0)
                reach(dve, a_ktlo, b, 1, 0)
                V.tensor_tensor(kt[:], psM[:, 1, 0:NG * LE].rearrange("p (g k) -> p g k", g=NG)[:, :, 0:LK],
                                bk_c[:].unsqueeze(2).broadcast_to([P, NG, LK]), ALU.add).then_inc(a_kt, 1)
                reach(dve, a_kthi, b, 1, 1)
                reach(dve, a_kt, b, 1, 1)
                reach(dve, a_kblo, b, 1, 0)
                V.tensor_tensor(kt2[:, 1], kt[:], f32(kt2[:, 0]), ALU.subtract).then_inc(a_ktlo, 1)

            def attend(b):
                for s in range(2 * NB):
                    t, blk = s // NB, s % NB
                    rs = slice(0, P if blk < NB - 1 else REST)
                    reach(dve, a_pThi, b, 6, s + 1)
                    V.tensor_tensor(pT[rs, 1, NG * blk:NG * (blk + 1), t * P:(t + 1) * P],
                                    psT[rs, s % 2, :].rearrange("p (g n) -> p g n", g=NG),
                                    f32(pT[rs, 0, NG * blk:NG * (blk + 1), t * P:(t + 1) * P]), ALU.subtract
                                    ).then_inc(a_pTlo, 1)
                reach(dve, a_otmp, b, 1, 1)
                reach(dve, a_ohi, b, 1, 0)
                reach(dve, a_olo, b, 1, 0)
                for r in range(2):
                    last = V.tensor_tensor(of[64 * r:64 * r + 64, :, :], psM[0:64, :, r * S:(r + 1) * S],
                                           otmp[:, :, r * S:(r + 1) * S], ALU.add)
                last.then_inc(a_of, 1)

            def values(b):
                reach(dve, a_v, b, 1, 1)
                reach(dve, a_vlo, b, 1, 0)
                V.tensor_tensor(vm[:], psT[:].rearrange("p a b -> p (a b)")[:, 0:NB * D].rearrange(
                                    "p (a j d) -> p a j d", j=HPG, d=DK),
                                mask[:, 1].unsqueeze(1).unsqueeze(3).broadcast_to([P, NB * NG, HPG, DK]), ALU.mult
                                ).then_inc(a_vm, 1)

            def iteration(i):
                last = isinstance(i.k, int)
                if not last or i.off + 1 < B:
                    norm_stats(i.plus(1))
                if not last or i.off < B:
                    for s in range(4):
                        shift(i, s)
                        if s == 1 and (not last or i.off + 1 < B):
                            norm(i.plus(1))
                    sums(i, 0)
                if not last or i.off >= 2:
                    residual(i.plus(-2))
                if not last or i.off < B:
                    sums(i, 1)
                if not last or i.off + 1 < B:
                    front(i.plus(1))
                if not last or 1 <= i.off <= B:
                    attend(i.plus(-1))
                if not last or i.off < B:
                    values(i)

            norm_stats(Step(0, 0))
            norm(Step(0, 0))
            split_weights()
            dve.wait_ge(w_zero, 4)
            dve.wait_ge(w_gain, 1)
            dve.wait_ge(w_bvwo, 1)
            V.tensor_tensor(bo_g[:], psT[:, 0, 0:D], bo_g[:], ALU.add).then_inc(w_bias, 1)
            dve.wait_ge(w_bias, 3)
            V.tensor_scalar(bo_g[:], bo_g[:], gains[:, 2:3], None, ALU.mult).then_inc(w_bias, 1)
            front(Step(0, 0))
            for i in range(PEEL):
                iteration(Step(0, i))
            with dve.Fori(0, (B - 1 - PEEL) // 2) as k:
                iteration(Step(k, PEEL))
                iteration(Step(k, PEEL + 1))
            for i in range(B - 1, B + 2):
                iteration(Step(0, i))

            def stats2(p):
                landed(dve, b_x, p)
                for t in range(TPP):
                    V.bn_stats(stats[:, t, :], x1p[:, p.parity, t, :]).then_inc(b_stat, 1)
                reach(dve, b_stat, p, TPP, TPP)
                V.memset(gate[:, 1:2], 0.0)
                for t in range(TPP):
                    last = V.bn_aggr(mv[:, t, :], stats[:, t, :])
                last.then_inc(b_mv, 1)

            def norm2(p):
                reach(dve, b_rstd, p, 1, 1)
                reach(dve, b_mv, p, 1, 1)
                reach(dve, b_xTp, p, 2, 0)
                for t in range(TPP):
                    last = V.tensor_scalar(xh2[:, t, :], x1p[:, p.parity, t, :], mv[:, t, 0:1], rstd[:, t:t + 1],
                                           ALU.subtract, ALU.mult)
                last.then_inc(b_xh, 1)

            def lo(p):
                for k in range(KD):
                    reach(dve, b_xThi, p, 2, k + 1)
                    V.tensor_tensor(x2T[:, p.parity, 1, k, :], psM[:, k, :], f32(x2T[:, p.parity, 0, k, :]),
                                    ALU.subtract).then_inc(b_xTlo, 1)

            def top2(p):
                reach(dve, b_lgt, p, 1, 1)
                V.tensor_copy(lg[:], psM[:, 1, 0:TPP * E].rearrange("p (t e) -> p t e", t=TPP)).then_inc(b_lg, 1)
                reach(dve, b_lg, p, 1, 1)
                V.memset(gate[:, 2:3], 0.0)
                for t in range(TPP):
                    last = V.max(top[:, t, :], lg[:, t, :])
                last.then_inc(b_top, 1)
                reach(dve, b_top, p, 1, 1)
                V.memset(gate[:, 3:4], 0.0)
                for t in range(TPP):
                    last = V.max_index(topi[:, t, :], top[:, t, :], lg[:, t, :])
                last.then_inc(b_topi, 1)
                V.tensor_tensor(ex[:], lg[:], top[:, :, 0:1].broadcast_to([P, TPP, E]), ALU.subtract
                                ).then_inc(b_sub, 1)
                reach(dve, b_topi, p, 1, 1)
                V.tensor_copy(topf[:], topi[:]).then_inc(b_topf, 1)
                reach(dve, b_topf, p, 1, 1)
                for n in range(2):
                    last = V.tensor_tensor(hot[:, n], iota[:].unsqueeze(1).broadcast_to([P, TPP, E]),
                                           topf[:, :, n:n + 1].broadcast_to([P, TPP, E]), ALU.is_equal)
                last.then_inc(b_hot, 1)

            def coefs(p):
                reach(dve, b_exp, p, 1, 1)
                V.tensor_reduce(esum[:], ex[:], AX.X, ALU.add).then_inc(b_sum, 1)
                reach(dve, b_hot, p, 1, 1)
                V.tensor_tensor(hot[:, 0], hot[:, 0], hot[:, 1], ALU.add).then_inc(b_sel, 1)
                reach(dve, b_sum, p, 1, 1)
                V.reciprocal(einv[:], esum[:]).then_inc(b_inv, 1)
                reach(dve, b_sel, p, 2, 1)
                V.tensor_tensor(ex[:], ex[:], hot[:, 0], ALU.mult).then_inc(b_sel, 1)
                reach(dve, b_inv, p, 1, 1)
                reach(dve, b_sel, p, 2, 2)
                V.tensor_tensor(ex[:], ex[:], einv[:].unsqueeze(2).broadcast_to([P, TPP, E]), ALU.mult
                                ).then_inc(b_cf, 1)
                reach(dve, b_cf, p, 2, 1)
                V.tensor_scalar(coef[:, p.parity], ex[:], gains[:, 3:4], None, ALU.mult).then_inc(b_cf, 1)

            def hidden(p, m):
                c = m % 2
                reach(dve, b_sil, p, NCH, m + 1)
                reach(dve, b_u, p, NCH, m + 1)
                reach(dve, b_hlo, p, NCH, m - 1)
                V.tensor_tensor(hf[:, c, :], psS[:, 2 * c + 1, :], sil[c], ALU.mult).then_inc(b_h, 1)
                reach(dve, b_hhi, p, NCH, m + 1)
                V.tensor_tensor(h2[:, c, 1, :], hf[:, c, :], f32(h2[:, c, 0, :]), ALU.subtract
                                ).then_inc(b_hlo, 1)

            def add_up(p, m):
                if m == 0:
                    return
                reach(dve, b_y, p, NCH, m + 1)
                reach(dve, b_acc, p, NCH - NSH + 1, m - 1)
                if m == NSH - 1:
                    acc = x1p[:, p.parity].rearrange("p (a b) c -> p a (b c)", a=2)
                    last = V.scalar_tensor_tensor(acc, psT[:], gains[:, 3:4], acc, ALU.mult, ALU.add)
                else:
                    reach(dve, b_cf, p, 2, 2)
                    for t in range(TPP):
                        last = V.scalar_tensor_tensor(
                            x1p[:, p.parity, t, :], psT[:, t // 2, (t % 2) * D:(t % 2 + 1) * D],
                            coef[:, p.parity, t, m - NSH:m - NSH + 1], x1p[:, p.parity, t, :],
                            ALU.mult, ALU.add)
                last.then_inc(b_acc, 1)

            def pair(p, prep, nxt):
                for m in range(NCH):
                    if m + 1 < NCH:
                        hidden(p, m + 1)
                    elif nxt:
                        hidden(p.plus(1), 0)
                    add_up(p, m)
                    if prep and m == 1:
                        stats2(p.plus(1))
                    if prep and m == 2:
                        norm2(p.plus(1))
                    if prep and m == 3:
                        lo(p.plus(1))
                    if prep and m == 5:
                        top2(p.plus(1))
                    if prep and m == 7:
                        coefs(p.plus(1))

            stats2(Step(0, 0))
            norm2(Step(0, 0))
            lo(Step(0, 0))
            top2(Step(0, 0))
            coefs(Step(0, 0))
            hidden(Step(0, 0), 0)
            pair(Step(0, 0), True, True)
            with dve.Fori(0, (NPAIR - 2) // 2) as k:
                pair(Step(k, 1), True, True)
                pair(Step(k, 2), True, True)
            pair(Step(0, NPAIR - 1), False, False)

        @block.gpsimd
        def _(pool):
            G = nc.gpsimd

            def inv_std(step, n, mv_done, eps_done, rstd_done):
                reach(pool, mv_done, step, 1, 1)
                G.tensor_tensor(rstd[:, 0:n], mv[:, 0:n, 1], eps[:, 0:n], ALU.add).then_inc(eps_done, 1)
                reach(pool, eps_done, step, 1, 1)
                G.tensor_tensor(rstd[:, 0:n], rstd[:, 0:n], half_neg[:, 0:n], ALU.pow).then_inc(rstd_done, 1)

            def normalise(i, t):
                reach(pool, a_rden, i, 2, t + 1)
                for g2 in range(0, NG, 2):
                    v = pr[:, i.parity, t, g2:g2 + 2].rearrange("p g (k j) -> p g k j", j=HPG)
                    last = G.tensor_tensor(v, v, rden[:, t, HPG * g2:HPG * (g2 + 2)].rearrange("p (g j) -> p g j", g=2
                                           ).unsqueeze(2).broadcast_to([P, 2, LK, HPG]), ALU.mult)
                last.then_inc(a_pn, 1)

            def bias(b):
                landed(pool, a_res, b)
                reach(pool, a_x1, b, 1, 0)
                G.tensor_tensor(xbias[:], xres[:, b.parity], bo_g[:].unsqueeze(1).broadcast_to([P, TPB, D]),
                                ALU.add).then_inc(a_xb, 1)

            def front(b):
                reach(pool, a_qhi, b, 1, 1)
                reach(pool, a_s, b, 4, 0)
                reach(pool, a_pn, b, 2, 0)
                for r in range(2):
                    rs, ro = slice(64 * r, 64 * r + 64), slice(64 * (1 - r), 64 * (1 - r) + 64)
                    G.tensor_tensor(qst[ro, r::2, :], qf[rs, :, :], f32(qst[rs, r::2, :]), ALU.subtract
                                    ).then_inc(a_qlo, 1)
                    reach(pool, a_qlo, b, 2, r + 1)
                reach(pool, a_kthi, b, 1, 1)
                G.tensor_tensor(kbd[:, 0].rearrange("p g k j -> p (g k) j"),
                                f32(kt2[:, 0]).rearrange("p g k -> p (g k)").unsqueeze(2).broadcast_to([P, NG * LK, HPG]),
                                mask[:, 0].unsqueeze(1).broadcast_to([P, NG * LK, HPG]), ALU.mult
                                ).then_inc(a_kbhi, 1)

            def attend(b):
                reach(pool, a_ohi, b, 1, 1)
                G.tensor_tensor(oT[:, 1], of[:], f32(oT[:, 0]), ALU.subtract).then_inc(a_olo, 1)

            def values(b):
                reach(pool, a_vhi, b, 1, 1)
                G.tensor_tensor(vbd[:, :, 1, :], vm[:].rearrange("p a j d -> p a (j d)"), f32(vbd[:, :, 0, :]),
                                ALU.subtract).then_inc(a_vlo, 1)

            def iteration(i):
                last = isinstance(i.k, int)
                if not last or i.off + 1 < B:
                    inv_std(i.plus(1), TPB, a_mv, a_eps, a_rstd)
                if not last or i.off >= 2:
                    bias(i.plus(-2))
                if not last or i.off < B:
                    normalise(i, 0)
                    normalise(i, 1)
                if not last or i.off + 1 < B:
                    front(i.plus(1))
                if not last or i.off < B:
                    values(i)
                if not last or 1 <= i.off <= B:
                    attend(i.plus(-1))

            pool.wait_ge(w_zero, 3)
            inv_std(Step(0, 0), TPB, a_mv, a_eps, a_rstd)
            front(Step(0, 0))
            pool.wait_ge(w_bias, 4)
            for i in range(PEEL):
                iteration(Step(0, i))
            with pool.Fori(0, (B - 1 - PEEL) // 2) as k:
                iteration(Step(k, PEEL))
                iteration(Step(k, PEEL + 1))
            for i in range(B - 1, B + 2):
                iteration(Step(0, i))

            inv_std(Step(0, 0), TPP, b_mv, b_eps, b_rstd)
            inv_std(Step(0, 1), TPP, b_mv, b_eps, b_rstd)
            with pool.Fori(0, (NPAIR - 2) // 2) as k:
                inv_std(Step(k, 2), TPP, b_mv, b_eps, b_rstd)
                inv_std(Step(k, 3), TPP, b_mv, b_eps, b_rstd)




_INS = ['x', 'ctx_512', 'g_xattn', 'g_ffn', 'L0_xattn_Wq', 'L0_xattn_bq', 'L0_xattn_Wk', 'L0_xattn_bk',
        'L0_xattn_Wv', 'L0_xattn_bv', 'L0_xattn_Wo', 'L0_xattn_bo', 'L0_ffn_router', 'L0_ffn_experts_gate',
        'L0_ffn_experts_up', 'L0_ffn_experts_down', 'L0_ffn_shared_gate', 'L0_ffn_shared_up',
        'L0_ffn_shared_down']


def kernel(**inputs):
    import numpy as np
    import concourse.bacc as bacc
    from concourse.bass_utils import run_bass_kernel_spmd

    nc = bacc.Bacc("TRN2", target_bir_lowering=False, num_devices=1)
    arrays = {name: np.ascontiguousarray(inputs[name]) for name in _INS}
    arrays["ident"] = np.eye(P, dtype=np.float32)
    row = np.arange(P)[:, None]
    arrays["head_masks"] = np.stack([row % (HPG * DK) // DK == np.arange(HPG), row % HPG == np.arange(HPG)],
                                    1).astype(np.float32)
    arrays["expert_numbers"] = np.tile(np.arange(E, dtype=np.float32), (P, 1))
    args = [nc.dram_tensor("in_" + n, a.shape, mybir.dt.from_np(a.dtype), kind="ExternalInput").ap()
            for n, a in arrays.items()]
    out = nc.dram_tensor("out", (B * S, D), F32, kind="ExternalOutput").ap()
    build(nc, *args, out)
    r = run_bass_kernel_spmd(nc, [{"in_" + n: a for n, a in arrays.items()}], core_ids=[0])
    return r.results[0]["out"].reshape(B, S, D)
```

```python
from contextlib import ExitStack

import concourse.bass as bass
from concourse import mybir

F32 = mybir.dt.float32
F32R = mybir.dt.float32r
U32 = mybir.dt.uint32
ALU = mybir.AluOpType
ACT = mybir.ActivationFunctionType
AX = mybir.AxisListType

P = 128
B, S, D = 32, 256, 256
LK, DC = 77, 128
HEADS, DK = 16, 16
NG, HPG = 4, 4
GW = HPG * LK
LE = LK + LK % 2
NB = -(-GW // P)
REST = GW - (NB - 1) * P
TPB = S // P
KD = D // P
E, DE, DS = 8, 128, 256
NCH = DS // P + E
NSH = DS // P
FW = NCH * P
PAIR = 2 * S
TPP = PAIR // P
NPAIR = B * S // PAIR
EPS = 1e-5
PEEL = 5
N_SMALL = 10
SCALE = DK ** -0.5


class Step:

    def __init__(self, k, off):
        self.k, self.off = k, off

    @property
    def index(self):
        return self.k * 2 + self.off

    @property
    def parity(self):
        return self.off % 2

    def plus(self, n):
        return Step(self.k, self.off + n)

    def count(self, per, n):
        return self.k * (2 * per) + (per * self.off + n)

    def has(self, per, n):
        assert isinstance(self.k, int) or per * self.off + n > 0, "a register may hold zero"
        return not isinstance(self.k, int) or self.count(per, n) > 0

    def exists(self):
        return self.has(1, 1)

    def loads(self, n=1):
        return self.k * (16 * n) + (self.off // 2 + 1) * (16 * n)


def f32(ap):
    return ap.bitcast(F32)


def build(nc, x, ctx_in, g_xattn, g_ffn, Wq, bq, Wk, bk, Wv, bv, Wo, bo, router,
          e_gate, e_up, e_down, s_gate, s_up, s_down, ident_in, mask_in, iota_in, out):
    with ExitStack() as ctx:
        def sb(name, shape, dt=F32):
            return ctx.enter_context(nc.sbuf_tensor(name, shape, dt))

        def sem(name):
            return ctx.enter_context(nc.semaphore(name))

        ident = sb("ident", [P, P])
        mask = sb("mask", [P, 2, HPG])
        iota = sb("iota", [P, E])
        gains = sb("gains", [P, 4])
        bq_c = sb("bq_c", [P, KD])
        bk_c = sb("bk_c", [P, NG])
        bv_c = sb("bv_c", [P, KD])
        bv_b = sb("bv_b", [P, 2, KD, P], F32R)
        bo_g = sb("bo_g", [P, D])
        half_neg = sb("half_neg", [P, TPP])
        eps = sb("eps", [P, TPP])
        gate = sb("gate", [P, 4])
        wq = sb("wq", [P, 2, KD, D], F32R)
        wk = sb("wk", [P, 2, NG, P], F32R)
        wv = sb("wv", [P, 2, D], F32R)
        wo = sb("wo", [P, 2, KD, D], F32R)
        wr = sb("wr", [P, 2, KD, P], F32R)
        wg = sb("wg", [P, 2, KD, FW], F32R)
        wu = sb("wu", [P, 2, KD, FW], F32R)
        wd = sb("wd", [P, 2, NCH, D], F32R)

        xin = sb("xin", [P, 2, TPB, D])
        cin = sb("cin", [LK, 2, DC])
        xres = sb("xres", [P, 2, TPB, D])
        xbias = sb("xbias", [P, TPB, D])
        x1b = sb("x1b", [P, 2, TPB, D])
        stats = sb("stats", [P, TPP, 6])
        mv = sb("mv", [P, TPP, 2])
        rstd = sb("rstd", [P, TPP])
        xh = sb("xh", [P, TPB, D])
        xT = sb("xT", [P, 2, KD, S], F32R)
        cT = sb("cT", [P, 2, 2, NB * P], F32R)
        qf = sb("qf", [P, KD, S])
        qst = sb("qst", [P, NG, S], F32R)
        kt = sb("kt", [P, NG, LK])
        kt2 = sb("kt2", [P, 2, NG, LK], F32R)
        kbd = sb("kbd", [P, 2, NG, LK, HPG], F32R)
        vm = sb("vm", [P, NB * NG, HPG, DK])
        vbd = sb("vbd", [P, NB * NG, 2, HPG * DK], F32R)
        pr = sb("pr", [P, 2, TPB, NG, GW])
        mx = sb("mx", [P, 2, HEADS // 2])
        den = sb("den", [P, TPB, HEADS])
        rden = sb("rden", [P, TPB, HEADS])
        pT = sb("pT", [P, 2, NB * NG, S], F32R)
        otmp = sb("otmp", [64, KD, 2 * S])
        of = sb("of", [P, KD, S])
        oT = sb("oT", [P, 2, KD, S], F32R)

        x2T = sb("x2T", [P, 2, 2, KD, PAIR], F32R)
        sil = [qf[:].rearrange("p a b -> p (a b)"), of[:].rearrange("p a b -> p (a b)")]

        taken = [0]

        def over_pr(*dims):
            n = 1
            for d in dims:
                n *= d
            taken[0] += n
            flat = pr[:].rearrange("p a t g n -> p (a t g n)")[:, taken[0] - n:taken[0]]
            names = "abc"[:len(dims)]
            return flat.rearrange(f"p ({' '.join(names)}) -> p {' '.join(names)}", **dict(zip(names, dims))) \
                if len(dims) > 1 else flat

        x1p = over_pr(2, TPP, D)
        xh2 = over_pr(TPP, D)
        hf = over_pr(2, PAIR)
        lgT = over_pr(PAIR)[0:E]
        lg = over_pr(TPP, E)
        top = over_pr(TPP, 8)
        topi = over_pr(TPP, 8).bitcast(U32)
        topf = over_pr(TPP, 8)
        ex = over_pr(TPP, E)
        hot = over_pr(2, TPP, E)
        esum = over_pr(TPP)
        einv = over_pr(TPP)
        coef = over_pr(2, TPP, E)
        h2 = pT[:].rearrange("p a b c -> p (a b c)")[:, 0:4 * PAIR].rearrange("p (a b c) -> p a b c", a=2, b=2)

        psS = ctx.enter_context(nc.psum_tensor("psS", [P, 4, 512], F32))
        psT = ctx.enter_context(nc.psum_tensor("psT", [P, 2, 512], F32))
        psM = ctx.enter_context(nc.psum_tensor("psM", [P, 2, 512], F32))

        turn_bank = [psT[:, 0], psT[:, 1], psT[:, 0], psM[:, 0], psM[:, 1], psT[:, 1]]
        x1_dram = nc.dram_tensor("x1_scratch", (B * S, D), F32, kind="Internal").ap()

        (w_in, w_hi, w_lo, w_zero, w_gain, w_bias, w_bvwo) = map(sem, (
            "w_in", "w_hi", "w_lo", "w_zero", "w_gain", "w_bias", "w_bvwo"))
        w_stage = [sem("w_stage0"), sem("w_stage1")]
        a_x = [sem("a_in0"), sem("a_in1")]
        a_res = [sem("a_res0"), sem("a_res1")]
        a_st = [sem("a_st0"), sem("a_st1")]
        (a_stat, a_mv, a_eps, a_rstd, a_xh, a_xTp, a_xThi, a_xTlo, a_cTp, a_cThi, a_cTlo, a_q, a_qf, a_qhi,
         a_qlo, a_k, a_kt, a_kthi, a_ktlo, a_kbhi, a_kblo, a_s, a_mx, a_sub, a_exp, a_den, a_rden, a_pn,
         a_pTp, a_pThi, a_pTlo, a_o, a_otmp, a_of, a_ohi, a_olo, a_v, a_vm, a_vhi, a_vlo, a_wo,
         a_xb, a_x1) = [sem("a_" + n) for n in (
            "stat mv eps rstd xh xTp xThi xTlo cTp cThi cTlo q qf qhi qlo k kt kthi ktlo kbhi kblo s mx "
            "sub exp den rden pn pTp pThi pTlo o otmp of ohi olo v vm vhi vlo wo xb x1").split()]
        b_x = [sem("b_x0"), sem("b_x1")]
        b_st = [sem("b_st0"), sem("b_st1")]
        (b_stat, b_mv, b_eps, b_rstd, b_xh, b_xTp, b_xThi, b_xTlo, b_lgp, b_lgT, b_lgt, b_lg, b_top, b_topi,
         b_topf, b_sub, b_exp, b_sum, b_inv, b_hot, b_sel, b_cf, b_g, b_u, b_sil, b_h, b_hhi, b_hlo, b_y,
         b_acc) = [sem("b_" + n) for n in (
            "stat mv eps rstd xh xTp xThi xTlo lgp lgT lgt lg top topi topf sub exp sum inv hot sel cf "
            "g u sil h hhi hlo y acc").split()]

        block = ctx.enter_context(nc.Block())

        stage = [pr[:, i].rearrange("p t g n -> p (t g n)") for i in range(2)]
        rows = lambda w: w.rearrange("(k p) n -> p k n", p=P)
        one = lambda t, i: t[:, i].rearrange("p a b -> p (a b)") if len(t.shape) == 4 else t[:, i]
        jobs = [([(rows(Wq), 0, (KD, D))], lambda i: one(wq, i), KD * D),
                ([(Wk.rearrange("p (g n) -> p g n", g=NG), 64 * r, (NG, P, 64)) for r in range(2)],
                 lambda i: one(wk, i), NG * P),
                ([(Wv, 0, None)], lambda i: wv[:, i], D),
                ([(rows(Wo), 0, (KD, D))], lambda i: one(wo, i), KD * D),
                ([(rows(router), 0, (KD, E))], lambda i: wr[:, i, :, 0:E], KD * E)]
        for w_s, w_e, target in ((s_gate, e_gate, wg), (s_up, e_up, wu)):
            for k in range(KD):
                jobs.append(([(w_s[k * P:(k + 1) * P, :], 0, None),
                              (w_e[:, k * P:(k + 1) * P, :].rearrange("e p d -> p e d"), DS, (E, DE))],
                             lambda i, k=k, target=target: target[:, i, k, :], FW))
        for h in range(2):
            n0, n1 = (0, 5) if h == 0 else (5, NCH)
            parts = ([(rows(s_down), 0, (NSH, D))] if h == 0 else [])
            m0 = NSH if h == 0 else n0
            parts.append((e_down[m0 - NSH:n1 - NSH].rearrange("e p d -> p e d"), (m0 - n0) * D, (n1 - m0, D)))
            jobs.append((parts, lambda i, n0=n0, n1=n1: wd[:, i, n0:n1, :].rearrange("p a b -> p (a b)"),
                         (n1 - n0) * D))

        def staged(n):
            parts, target, width = jobs[n]
            v = stage[n % 2][:, 0:width]
            return v.rearrange("p (a b) -> p a b", a=KD) if n == 4 else v

        job_parts = [sum(len(j[0]) for j in jobs[n % 2:n + 1:2]) for n in range(len(jobs))]

        @block.sync
        def _(sp):
            def load_x(b):
                if b.has(1, -1):
                    sp.wait_ge(a_xh, b.count(1, -1))
                if b.has(1, -1):
                    sp.wait_ge(a_cTp, b.count(1, -1))
                sp.dma_start(xin[:, b.parity], x[b.index].rearrange("(t p) d -> p t d", p=P)
                             ).then_inc(a_x[b.parity], 16)
                sp.dma_start(cin[:, b.parity], ctx_in[b.index]).then_inc(a_x[b.parity], 16)

            def load_res(b):
                if b.has(1, -1):
                    sp.wait_ge(a_xb, b.count(1, -1))
                sp.dma_start(xres[:, b.parity], x[b.index].rearrange("(t p) d -> p t d", p=P)
                             ).then_inc(a_res[b.parity], 16)

            def store_x1(b):
                sp.wait_ge(a_x1, b.count(1, 1))
                sp.dma_start(x1_dram[bass.ds(b.index * S, S), :].rearrange("(t p) d -> p t d", p=P),
                             x1b[:, b.parity]).then_inc(a_st[b.parity], 16)

            def load_x1(p):
                if p.plus(-2).exists():
                    sp.wait_ge(b_st[p.plus(-2).parity], p.plus(-2).loads())
                sp.dma_start(x1p[:, p.parity],
                             x1_dram[bass.ds(p.index * PAIR, PAIR), :].rearrange("(t p) d -> p t d", p=P)
                             ).then_inc(b_x[p.parity], 16)

            def store_out(p):
                if p.has(NCH - NSH + 1, NCH - NSH + 1):
                    sp.wait_ge(b_acc, p.count(NCH - NSH + 1, NCH - NSH + 1))
                sp.dma_start(out[bass.ds(p.index * PAIR, PAIR), :].rearrange("(t p) d -> p t d", p=P),
                             x1p[:, p.parity]).then_inc(b_st[p.parity], 16)

            load_x(Step(0, 0))
            small = [(ident[:], ident_in), (mask[:], mask_in), (iota[:], iota_in),
                     (gains[:, 0:1], g_xattn.rearrange("(a b) -> a b", a=1).partition_broadcast(P)),
                     (gains[:, 1:2], g_ffn.rearrange("(a b) -> a b", a=1).partition_broadcast(P)),
                     (bq_c[:], bq.rearrange("(m p) -> p m", p=P)),
                     (bk_c[0:64, :], bk.rearrange("(g p) -> p g", p=64)),
                     (bk_c[64:P, :], bk.rearrange("(g p) -> p g", p=64)),
                     (bv_c[:], bv.rearrange("(m p) -> p m", p=P)),
                     (bo_g[:], bo.rearrange("(a b) -> a b", a=1).partition_broadcast(P))]
            for dst, src in small:
                sp.dma_start(dst, src, allow_slow_non_contiguous=True).then_inc(w_in, 16)
            for n, (parts, target, width) in enumerate(jobs):
                if n >= 2:
                    sp.wait_ge(w_lo, n - 1)
                for src, at, dims in parts:
                    dst = stage[n % 2]
                    if dims is None:
                        dst = dst[:, at:at + src.shape[1]]
                    elif len(dims) == 2:
                        dst = dst[:, at:at + dims[0] * dims[1]].rearrange("p (a b) -> p a b", a=dims[0])
                    else:
                        dst = dst[:, 0:dims[0] * dims[1]].rearrange("p (a b) -> p a b", a=dims[0])[
                            :, :, at:at + dims[2]]
                    sp.dma_start(dst, src).then_inc(w_stage[n % 2], 16)
            load_x(Step(0, 1))

            def iteration(i):
                last = isinstance(i.k, int)
                if not last or i.off + 2 < B:
                    load_x(i.plus(2))
                if not last or 1 <= i.off <= B:
                    load_res(i.plus(-1))
                if not last or i.off >= 2:
                    store_x1(i.plus(-2))

            for i in range(PEEL):
                iteration(Step(0, i))
            with sp.Fori(0, (B - 3 - PEEL) // 2) as k:
                iteration(Step(k, PEEL))
                iteration(Step(k, PEEL + 1))
            for i in range(B - 3, B + 2):
                iteration(Step(0, i))

            sp.wait_ge(a_st[Step(0, B - 2).parity], Step(0, B - 2).loads())
            sp.wait_ge(a_st[Step(0, B - 1).parity], Step(0, B - 1).loads())
            load_x1(Step(0, 0))
            load_x1(Step(0, 1))
            store_out(Step(0, 0))
            with sp.Fori(0, (NPAIR - 2) // 2) as k:
                for off in (1, 2):
                    load_x1(Step(k, off + 1))
                    store_out(Step(k, off))
            store_out(Step(0, NPAIR - 1))
            sp.wait_ge(b_st[Step(0, NPAIR - 2).parity], Step(0, NPAIR - 2).loads())
            sp.wait_ge(b_st[Step(0, NPAIR - 1).parity], Step(0, NPAIR - 1).loads())

        @block.tensor
        def _(pe):
            mm = nc.tensor.matmul

            def scores(i, steps):
                for s in steps:
                    t, hh = s // 2, s % 2
                    if s == 0:
                        pe.wait_ge(a_qhi, i.count(1, 1))
                        pe.wait_ge(a_qlo, i.count(2, 2))
                        pe.wait_ge(a_kbhi, i.count(1, 1))
                        pe.wait_ge(a_kblo, i.count(1, 1))
                    if i.has(4, s - 1):
                        pe.wait_ge(a_sub, i.count(4, s - 1))
                    for g2 in range(2):
                        g = 2 * hh + g2
                        for part in range(2):
                            last = mm(psS[:, 2 * (s % 2) + g2, 0:GW], qst[:, g, t * P:(t + 1) * P],
                                      kbd[:, part, g].rearrange("p k j -> p (k j)"),
                                      start=(part == 0), stop=(part == 1))
                    last.then_inc(a_s, 1)

            def out_proj(i):
                pe.wait_ge(a_ohi, i.count(1, 1))
                pe.wait_ge(a_olo, i.count(1, 1))
                if isinstance(i.k, int) and 2 * i.k + i.off == B - 1:
                    pe.wait_ge(a_pTlo, i.count(6, 6))
                else:
                    pe.wait_ge(a_pTlo, i.plus(1).count(6, 2))
                for t in range(TPB):
                    n = 0
                    for m in range(KD):
                        for a, w in ((0, 0), (0, 1), (1, 0)):
                            last = mm(psT[:, 1, t * D:(t + 1) * D], oT[:, a, m, t * P:(t + 1) * P],
                                      wo[:, w, m, :], start=(n == 0), stop=(n == 5))
                            n += 1
                last.then_inc(a_wo, 1)

            def turn_x(b):
                pe.wait_ge(a_xh, b.count(1, 1))
                if b.has(1, -2):
                    pe.wait_ge(a_otmp, b.count(1, -2))
                if b.has(1, -2):
                    pe.wait_ge(a_of, b.count(1, -2))
                for k in range(KD):
                    for t in range(TPB):
                        last = nc.tensor.transpose(psM[:, 0, k * S + t * P:k * S + (t + 1) * P],
                                                   xh[:, t, k * P:(k + 1) * P], ident[:])
                last.then_inc(a_xTp, 1)
                pe.wait_ge(a_x[b.parity], b.loads(2))
                nc.tensor.transpose(psM[:, 1, 0:LK], cin[:, b.parity], ident[0:LK, 0:LK]).then_inc(a_cTp, 1)

            def queries(b):
                pe.wait_ge(a_xThi, b.count(1, 1))
                pe.wait_ge(a_xTlo, b.count(1, 1))
                for m in range(KD):
                    n = 0
                    for k in range(KD):
                        for w, a in ((0, 0), (1, 0), (0, 1)):
                            last = mm(psM[:, 0, m * S:(m + 1) * S], wq[:, w, k, m * P:(m + 1) * P],
                                      xT[:, a, k, :], start=(n == 0), stop=(n == 5))
                            n += 1
                last.then_inc(a_q, 1)

            def keys(b):
                pe.wait_ge(a_cThi, b.count(1, 1))
                pe.wait_ge(a_cTlo, b.count(1, 1))
                for g in range(NG):
                    for n, (w, a) in enumerate(((0, 0), (1, 0), (0, 1))):
                        last = mm(psM[:, 1, g * LE:(g + 1) * LE], wk[:, w, g, :], cT[:, b.parity, a, 0:LE * HPG:HPG],
                                  start=(n == 0), stop=(n == 2))
                last.then_inc(a_k, 1)

            def values(b):
                pe.wait_ge(a_cThi, b.count(1, 1))
                pe.wait_ge(a_cTlo, b.count(1, 1))
                if b.plus(-1).has(6, 6):
                    pe.wait_ge(a_pTlo, b.plus(-1).count(6, 6))
                for blk in range(NB):
                    for n, (a, w) in enumerate(((0, 0), (0, 1), (1, 0))):
                        last = mm(psT[:, blk // 2, (blk % 2) * D:(blk % 2 + 1) * D],
                                  cT[:, b.parity, a, blk * P:(blk + 1) * P], wv[:, w, :], start=(n == 0), stop=(n == 2))
                last.then_inc(a_v, 1)

            def turn_p(b, steps, read=None):
                for s in steps:
                    t, blk = s // NB, s % NB
                    rows_of = P if blk < NB - 1 else REST
                    if blk == 0:
                        pe.wait_ge(a_pn, b.count(2, t + 1))
                    if s < 2:
                        pe.wait_ge(a_vm, b.count(1, 1))
                    if s == 3:
                        if read.has(1, 1):
                            pe.wait_ge(a_qf, read.count(1, 1))
                    if s == 4:
                        if read.has(1, 1):
                            pe.wait_ge(a_kt, read.count(1, 1))
                    for g in range(NG):
                        if blk == NB - 2 and g == NG - 1:
                            if s == 1:
                                pe.wait_ge(a_pTlo, b.count(6, 1))
                            else:
                                if b.has(1, 0):
                                    pe.wait_ge(a_x1, b.count(1, 0))
                        last = nc.tensor.transpose(turn_bank[s][0:rows_of, g * P:(g + 1) * P],
                                                   pr[:, b.parity, t, g, blk * P:blk * P + rows_of], ident[:])
                    last.then_inc(a_pTp, 1)

            def attend(b):
                pe.wait_ge(a_pThi, b.count(6, 6))
                pe.wait_ge(a_pTlo, b.count(6, 6))
                pe.wait_ge(a_vhi, b.count(1, 1))
                pe.wait_ge(a_vlo, b.count(1, 1))
                for g in range(NG):
                    n = 0
                    for blk in range(NB):
                        for part in range(2):
                            last = mm(psM[:, g // 2, (g % 2) * S:(g % 2 + 1) * S],
                                      vbd[:, blk * NG + g].rearrange("p a b -> p (a b)"),
                                      pT[:, part, blk * NG + g, :], start=(n == 0), stop=(n == 2 * NB - 1))
                            n += 1
                last.then_inc(a_o, 1)

            def iteration(i):
                inner = not isinstance(i.k, int)
                now, nxt = inner or i.off < B, inner or i.off + 1 < B
                past, out_of = inner or 1 <= i.off <= B, inner or i.off >= 2
                if now:
                    scores(i, (0, 1))
                if nxt:
                    turn_x(i.plus(1))
                if past:
                    turn_p(i.plus(-1), (0, 1))
                if now:
                    scores(i, (2,))
                if nxt:
                    queries(i.plus(1))
                if past:
                    turn_p(i.plus(-1), (2,))
                if now:
                    scores(i, (3,))
                if out_of:
                    out_proj(i.plus(-2))
                if nxt:
                    keys(i.plus(1))
                if past:
                    turn_p(i.plus(-1), (3, 4, 5), i.plus(1) if nxt else Step(0, B - 1))
                    attend(i.plus(-1))
                if now:
                    values(i)

            pe.wait_ge(w_lo, 2)
            pe.wait_ge(w_hi, 2)
            pe.wait_ge(w_in, 16 * N_SMALL)
            pe.wait_ge(w_lo, len(jobs))
            pe.wait_ge(w_bias, 2)
            n = 0
            for m in range(KD):
                for a, w in ((0, 0), (0, 1), (1, 0)):
                    last = mm(psT[:, 0, 0:D], bv_b[:, a, m, :], wo[:, w, m, :], start=(n == 0), stop=(n == 5))
                    n += 1
            last.then_inc(w_bvwo, 1)
            turn_x(Step(0, 0))
            queries(Step(0, 0))
            keys(Step(0, 0))
            for i in range(PEEL):
                iteration(Step(0, i))
            with pe.Fori(0, (B - 3 - PEEL) // 2) as k:
                iteration(Step(k, PEEL))
                iteration(Step(k, PEEL + 1))
            for i in range(B - 3, B + 2):
                iteration(Step(0, i))

            def transposes(p):
                pe.wait_ge(b_xh, p.count(1, 1))
                if p.has(1, 0):
                    pe.wait_ge(b_lg, p.count(1, 0))
                for k in range(KD):
                    for t in range(TPP):
                        last = nc.tensor.transpose(psM[:, k, t * P:(t + 1) * P],
                                                   xh2[:, t, k * P:(k + 1) * P], ident[:])
                    last.then_inc(b_xTp, 1)

            def route(p):
                pe.wait_ge(b_xThi, p.count(2, 2))
                pe.wait_ge(b_xTlo, p.count(2, 2))
                n = 0
                for k in range(KD):
                    for w, a in ((0, 0), (1, 0), (0, 1)):
                        last = mm(psM[:, 0, :], wr[:, w, k, :], x2T[:, p.parity, a, k, :],
                                  start=(n == 0), stop=(n == 5))
                        n += 1
                last.then_inc(b_lgp, 1)

            def route_back(p):
                if isinstance(p.k, int):
                    pe.wait_ge(b_lgT, p.count(1, 1))
                for t in range(TPP):
                    last = nc.tensor.transpose(psM[:, 1, t * E:(t + 1) * E], lgT[:, t * P:(t + 1) * P],
                                               ident[0:E, 0:E])
                last.then_inc(b_lgt, 1)

            def gate_up(p, m):
                c = m % 2
                if p.has(NCH, m - 1):
                    pe.wait_ge(b_h, p.count(NCH, m - 1))
                for w2, base, done in ((wg, 0, b_g), (wu, 1, b_u)):
                    n = 0
                    for k in range(KD):
                        for w, a in ((0, 0), (1, 0), (0, 1)):
                            last = mm(psS[:, 2 * c + base, :], w2[:, w, k, m * P:(m + 1) * P],
                                      x2T[:, p.parity, a, k, :], start=(n == 0), stop=(n == 5))
                            n += 1
                    last.then_inc(done, 1)

            def down(p, m, ahead=False):
                c = m % 2
                pe.wait_ge(b_hhi, p.count(NCH, m + 1))
                pe.wait_ge(b_hlo, p.count(NCH, m + 1))
                if m != 1:
                    if p.has(NCH - NSH + 1, max(m - 1, 0)):
                        pe.wait_ge(b_acc, p.count(NCH - NSH + 1, max(m - 1, 0)))
                for t in range(TPP):
                    if ahead and t == TPP - 1:
                        pe.wait_ge(b_lgT, p.plus(1).count(1, 1))
                    for n, (a, w) in enumerate(((0, 0), (0, 1), (1, 0))):
                        if m < NSH:
                            start = m == 0 and n == 0 and t % 2 == 0
                            stop = m == NSH - 1 and n == 2
                        else:
                            start, stop = n == 0, n == 2
                        last = mm(psT[:, t // 2, (t % 2) * D:(t % 2 + 1) * D],
                                  h2[:, c, a, t * P:(t + 1) * P], wd[:, w, m, :],
                                  start=start, stop=stop, skip_group_check=(m < NSH))
                last.then_inc(b_y, 1)

            def pair(p, prep, nxt):
                for m in range(NCH):
                    if m + 1 < NCH:
                        gate_up(p, m + 1)
                    elif nxt:
                        gate_up(p.plus(1), 0)
                    down(p, m, prep and m == 5)
                    if prep and m == 3:
                        transposes(p.plus(1))
                    if prep and m == 4:
                        route(p.plus(1))
                    if prep and m == 5:
                        route_back(p.plus(1))

            transposes(Step(0, 0))
            route(Step(0, 0))
            route_back(Step(0, 0))
            gate_up(Step(0, 0), 0)
            pair(Step(0, 0), True, True)
            with pe.Fori(0, (NPAIR - 2) // 2) as k:
                pair(Step(k, 1), True, True)
                pair(Step(k, 2), True, True)
            pair(Step(0, NPAIR - 1), False, False)

        @block.scalar
        def _(act):
            act.wait_ge(w_in, 16 * N_SMALL)
            nc.scalar.activation(gains[:, 2:4], gains[:, 0:2], ACT.Tanh).then_inc(w_gain, 1)
            for n, (parts, target, width) in enumerate(jobs):
                act.wait_ge(w_stage[n % 2], 16 * job_parts[n])
                if n == 4:
                    act.wait_ge(w_zero, 1)
                nc.scalar.copy(target(0), staged(n)).then_inc(w_hi, 1)

            def front_x(b):
                act.wait_ge(a_xTp, b.count(1, 1))
                if b.has(1, 0):
                    act.wait_ge(a_q, b.count(1, 0))
                nc.scalar.copy(xT[:, 0].rearrange("p a b -> p (a b)"), psM[:, 0, :]).then_inc(a_xThi, 1)
                act.wait_ge(a_cTp, b.count(1, 1))
                if b.has(1, -1):
                    act.wait_ge(a_v, b.count(1, -1))
                nc.scalar.copy(cT[:, b.parity, 0, 0:GW].rearrange("p (k j) -> p k j", j=HPG),
                               psM[:, 1, 0:LK].unsqueeze(2).broadcast_to([P, LK, HPG])).then_inc(a_cThi, 1)

            def front_q(b):
                act.wait_ge(a_q, b.count(1, 1))
                if b.has(2, 0):
                    act.wait_ge(a_qlo, b.count(2, 0))
                for m in range(KD):
                    last = nc.scalar.activation(qf[:, m, :], psM[:, 0, m * S:(m + 1) * S], ACT.Identity,
                                                bias=bq_c[:, m:m + 1])
                last.then_inc(a_qf, 1)

            def front_qhi(b):
                if b.has(4, 0):
                    act.wait_ge(a_s, b.count(4, 0))
                act.wait_ge(a_qf, b.count(1, 1))
                for r in range(2):
                    rs = slice(64 * r, 64 * r + 64)
                    last = nc.scalar.copy(qst[rs, r::2, :], qf[rs, :, :])
                last.then_inc(a_qhi, 1)

            def front_k(b):
                act.wait_ge(a_kt, b.count(1, 1))
                if b.has(1, 0):
                    act.wait_ge(a_kbhi, b.count(1, 0))
                nc.scalar.copy(kt2[:, 0], kt[:]).then_inc(a_kthi, 1)

            def front_kb(b):
                act.wait_ge(a_ktlo, b.count(1, 1))
                if b.has(4, 0):
                    act.wait_ge(a_s, b.count(4, 0))
                for j in range(HPG):
                    last = nc.scalar.activation(kbd[:, 1, :, :, j], f32(kt2[:, 1]), ACT.Copy,
                                                scale=mask[:, 0, j:j + 1])
                last.then_inc(a_kblo, 1)

            def exps(i, s):
                t, hh = s // 2, s % 2
                act.wait_ge(a_sub, i.count(4, s + 1))
                v = pr[:, i.parity, t, 2 * hh:2 * hh + 2, :]
                nc.scalar.activation(v, v, ACT.Exp, scale=SCALE).then_inc(a_exp, 1)

            def turned(b, steps):
                for s in steps:
                    t, blk = s // NB, s % NB
                    rs = slice(0, P if blk < NB - 1 else REST)
                    act.wait_ge(a_pTp, b.count(6, s + 1))
                    if s == 0:
                        if b.has(1, 0):
                            act.wait_ge(a_o, b.count(1, 0))
                    nc.scalar.copy(pT[rs, 0, NG * blk:NG * (blk + 1), t * P:(t + 1) * P],
                                   turn_bank[s][rs].rearrange("p (g n) -> p g n", g=NG)).then_inc(a_pThi, 1)

            def attended(b):
                act.wait_ge(a_o, b.count(1, 1))
                if b.has(1, 0):
                    act.wait_ge(a_of, b.count(1, 0))
                nc.scalar.copy(otmp[:], psM[64:P, :, :]).then_inc(a_otmp, 1)

            def attend_hi(b):
                act.wait_ge(a_of, b.count(1, 1))
                if b.has(1, 0):
                    act.wait_ge(a_wo, b.count(1, 0))
                nc.scalar.copy(oT[:, 0], of[:]).then_inc(a_ohi, 1)

            def values(b):
                act.wait_ge(a_vm, b.count(1, 1))
                if b.has(1, 0):
                    act.wait_ge(a_o, b.count(1, 0))
                nc.scalar.copy(vbd[:, :, 0, :], vm[:].rearrange("p a j d -> p a (j d)")).then_inc(a_vhi, 1)

            def iteration(i):
                inner = not isinstance(i.k, int)
                now, nxt = inner or i.off < B, inner or i.off + 1 < B
                past, out_of = inner or 1 <= i.off <= B, inner or i.off >= 2
                if now:
                    exps(i, 0)
                    exps(i, 1)
                if out_of:
                    attend_hi(i.plus(-2))
                if past:
                    values(i.plus(-1))
                if nxt:
                    front_x(i.plus(1))
                if past:
                    turned(i.plus(-1), (0, 1))
                if now:
                    exps(i, 2)
                if nxt:
                    front_q(i.plus(1))
                if past:
                    turned(i.plus(-1), (2,))
                if now:
                    exps(i, 3)
                if nxt:
                    front_qhi(i.plus(1))
                    front_k(i.plus(1))
                if past:
                    turned(i.plus(-1), (3, 4, 5))
                if nxt:
                    front_kb(i.plus(1))
                if past:
                    attended(i.plus(-1))

            act.wait_ge(w_zero, 5)
            front_x(Step(0, 0))
            front_q(Step(0, 0))
            front_k(Step(0, 0))
            front_qhi(Step(0, 0))
            front_kb(Step(0, 0))
            for i in range(PEEL):
                iteration(Step(0, i))
            with act.Fori(0, (B - 3 - PEEL) // 2) as k:
                iteration(Step(k, PEEL))
                iteration(Step(k, PEEL + 1))
            for i in range(B - 3, B + 2):
                iteration(Step(0, i))

            def hi(p):
                for k in range(KD):
                    act.wait_ge(b_xTp, p.count(2, k + 1))
                    nc.scalar.copy(x2T[:, p.parity, 0, k, :], psM[:, k, :]).then_inc(b_xThi, 1)

            def logits(p):
                act.wait_ge(b_lgp, p.count(1, 1))
                if p.has(1, 0):
                    act.wait_ge(b_lgt, p.count(1, 0))
                nc.scalar.copy(lgT[:], psM[0:E, 0, :]).then_inc(b_lgT, 1)

            def exp(p):
                act.wait_ge(b_sub, p.count(1, 1))
                nc.scalar.activation(ex[:], ex[:], ACT.Exp).then_inc(b_exp, 1)

            def chunk(p, m):
                act.wait_ge(b_g, p.count(NCH, m + 1))
                if p.has(NCH, m - 1):
                    act.wait_ge(b_h, p.count(NCH, m - 1))
                nc.scalar.activation(sil[m % 2], psS[:, 2 * (m % 2), :], ACT.Silu).then_inc(b_sil, 1)
                act.wait_ge(b_h, p.count(NCH, m + 1))
                if p.has(NCH, m - 1):
                    act.wait_ge(b_y, p.count(NCH, m - 1))
                nc.scalar.copy(h2[:, m % 2, 0, :], hf[:, m % 2, :]).then_inc(b_hhi, 1)

            def pair(p, prep):
                for m in range(NCH):
                    chunk(p, m)
                    if prep and m == 4:
                        hi(p.plus(1))
                    if prep and m == 5:
                        logits(p.plus(1))
                    if prep and m == 7:
                        exp(p.plus(1))

            hi(Step(0, 0))
            logits(Step(0, 0))
            exp(Step(0, 0))
            pair(Step(0, 0), True)
            with act.Fori(0, (NPAIR - 2) // 2) as k:
                pair(Step(k, 1), True)
                pair(Step(k, 2), True)
            pair(Step(0, NPAIR - 1), False)

        @block.vector
        def _(dve):
            V = nc.vector
            V.memset(f32(wr[:]), 0.0).then_inc(w_zero, 1)
            V.memset(eps[:], EPS).then_inc(w_zero, 1)
            V.memset(half_neg[:], -0.5).then_inc(w_zero, 1)
            V.memset(f32(pT[:]), 0.0).then_inc(w_zero, 1)
            V.memset(f32(cT[:]), 0.0).then_inc(w_zero, 1)
            dve.wait_ge(w_in, 16 * N_SMALL)
            bv_cols = bv_c[:].unsqueeze(2).broadcast_to([P, KD, P])
            V.tensor_copy(bv_b[:, 0], bv_cols).then_inc(w_bias, 1)
            dve.wait_ge(w_bias, 1)
            V.tensor_tensor(bv_b[:, 1], bv_cols, f32(bv_b[:, 0]), ALU.subtract).then_inc(w_bias, 1)

            def stats_of(b, src, done):
                for t in range(TPB):
                    V.bn_stats(stats[:, t, :], src[:, t, :]).then_inc(a_stat, 1)
                dve.wait_ge(a_stat, b.count(TPB, TPB))
                V.memset(gate[:, 0:1], 0.0)
                for t in range(TPB):
                    last = V.bn_aggr(mv[:, t, :], stats[:, t, :])
                last.then_inc(done, 1)

            def norm_stats(b):
                dve.wait_ge(a_x[b.parity], b.loads(2))
                stats_of(b, xin[:, b.parity], a_mv)

            def norm(b):
                dve.wait_ge(a_rstd, b.count(1, 1))
                dve.wait_ge(a_mv, b.count(1, 1))
                if b.has(1, 0):
                    dve.wait_ge(a_xTp, b.count(1, 0))
                for t in range(TPB):
                    last = V.tensor_scalar(xh[:, t, :], xin[:, b.parity, t, :], mv[:, t, 0:1], rstd[:, t:t + 1],
                                           ALU.subtract, ALU.mult)
                last.then_inc(a_xh, 1)

            def split_weights():
                for n, (parts, target, width) in enumerate(jobs):
                    dve.wait_ge(w_hi, n + 1)
                    V.tensor_tensor(target(1), staged(n), f32(target(0)), ALU.subtract
                                    ).then_inc(w_lo, 1)
                dve.wait_ge(w_lo, len(jobs))

            def shift(i, s):
                t, hh = s // 2, s % 2
                dve.wait_ge(a_s, i.count(4, s + 1))
                bank = psS[:, 2 * (s % 2):2 * (s % 2) + 2, 0:GW]
                if i.has(4, s - 1):
                    dve.wait_ge(a_sub, i.count(4, s - 1))
                V.tensor_reduce(mx[:, s % 2, :], bank.rearrange("p g (k j) -> p g j k", j=HPG), AX.X, ALU.max
                                ).then_inc(a_mx, 1)
                dve.wait_ge(a_mx, i.count(4, s + 1))
                if s == 0:
                    if i.has(6, -6):
                        dve.wait_ge(a_pTp, i.count(6, -6))
                V.tensor_tensor(
                    pr[:, i.parity, t, 2 * hh:2 * hh + 2, :].rearrange("p g (k j) -> p g k j", j=HPG),
                    bank.rearrange("p g (k j) -> p g k j", j=HPG),
                    mx[:, s % 2, :].rearrange("p (g j) -> p g j", g=2).unsqueeze(2).broadcast_to([P, 2, LK, HPG]),
                    ALU.subtract).then_inc(a_sub, 1)

            def sums(i, t):
                dve.wait_ge(a_exp, i.count(4, 2 * t + 2))
                if i.has(2, t - 1):
                    dve.wait_ge(a_rden, i.count(2, t - 1))
                V.tensor_reduce(den[:, t, :], pr[:, i.parity, t].rearrange("p g (k j) -> p g j k", j=HPG),
                                AX.X, ALU.add).then_inc(a_den, 1)
                dve.wait_ge(a_den, i.count(2, t + 1))
                if i.has(2, t - 1):
                    dve.wait_ge(a_pn, i.count(2, t - 1))
                V.reciprocal(rden[:, t, :], den[:, t, :]).then_inc(a_rden, 1)

            def residual(i):
                dve.wait_ge(a_wo, i.count(1, 1))
                dve.wait_ge(a_xb, i.count(1, 1))
                if i.plus(-2).exists():
                    dve.wait_ge(a_st[i.plus(-2).parity], i.plus(-2).loads())
                V.scalar_tensor_tensor(x1b[:, i.parity].rearrange("p a b -> p (a b)"), psT[:, 1, :],
                                       gains[:, 2:3], xbias[:].rearrange("p a b -> p (a b)"),
                                       ALU.mult, ALU.add).then_inc(a_x1, 1)

            def front(b):
                dve.wait_ge(a_xThi, b.count(1, 1))
                V.tensor_tensor(xT[:, 1].rearrange("p a b -> p (a b)"), psM[:, 0, :],
                                f32(xT[:, 0]).rearrange("p a b -> p (a b)"), ALU.subtract).then_inc(a_xTlo, 1)
                dve.wait_ge(a_cThi, b.count(1, 1))
                V.tensor_tensor(cT[:, b.parity, 1, 0:GW].rearrange("p (k j) -> p k j", j=HPG),
                                psM[:, 1, 0:LK].unsqueeze(2).broadcast_to([P, LK, HPG]),
                                f32(cT[:, b.parity, 0, 0:GW]).rearrange("p (k j) -> p k j", j=HPG), ALU.subtract
                                ).then_inc(a_cTlo, 1)

            def front_k(b):
                dve.wait_ge(a_k, b.count(1, 1))
                if b.has(1, 0):
                    dve.wait_ge(a_kthi, b.count(1, 0))
                if b.has(1, 0):
                    dve.wait_ge(a_ktlo, b.count(1, 0))
                V.tensor_tensor(kt[:], psM[:, 1, 0:NG * LE].rearrange("p (g k) -> p g k", g=NG)[:, :, 0:LK],
                                bk_c[:].unsqueeze(2).broadcast_to([P, NG, LK]), ALU.add).then_inc(a_kt, 1)
                dve.wait_ge(a_kthi, b.count(1, 1))
                dve.wait_ge(a_kt, b.count(1, 1))
                if b.has(1, 0):
                    dve.wait_ge(a_kblo, b.count(1, 0))
                V.tensor_tensor(kt2[:, 1], kt[:], f32(kt2[:, 0]), ALU.subtract).then_inc(a_ktlo, 1)

            def turned(b, steps):
                for s in steps:
                    t, blk = s // NB, s % NB
                    rs = slice(0, P if blk < NB - 1 else REST)
                    dve.wait_ge(a_pThi, b.count(6, s + 1))
                    V.tensor_tensor(pT[rs, 1, NG * blk:NG * (blk + 1), t * P:(t + 1) * P],
                                    turn_bank[s][rs].rearrange("p (g n) -> p g n", g=NG),
                                    f32(pT[rs, 0, NG * blk:NG * (blk + 1), t * P:(t + 1) * P]), ALU.subtract
                                    ).then_inc(a_pTlo, 1)

            def attended(b):
                dve.wait_ge(a_otmp, b.count(1, 1))
                if b.has(1, 0):
                    dve.wait_ge(a_ohi, b.count(1, 0))
                if b.has(1, 0):
                    dve.wait_ge(a_olo, b.count(1, 0))
                for r in range(2):
                    last = V.tensor_tensor(of[64 * r:64 * r + 64, :, :], psM[0:64, :, r * S:(r + 1) * S],
                                           otmp[:, :, r * S:(r + 1) * S], ALU.add)
                last.then_inc(a_of, 1)

            def values(b):
                dve.wait_ge(a_v, b.count(1, 1))
                if b.has(1, 0):
                    dve.wait_ge(a_vlo, b.count(1, 0))
                V.tensor_tensor(vm[:], psT[:].rearrange("p a b -> p (a b)")[:, 0:NB * D].rearrange(
                                    "p (a j d) -> p a j d", j=HPG, d=DK),
                                mask[:, 1].unsqueeze(1).unsqueeze(3).broadcast_to([P, NB * NG, HPG, DK]), ALU.mult
                                ).then_inc(a_vm, 1)

            def iteration(i):
                inner = not isinstance(i.k, int)
                now, nxt = inner or i.off < B, inner or i.off + 1 < B
                past, out_of = inner or 1 <= i.off <= B, inner or i.off >= 2
                after = inner or i.off + 2 < B
                if now:
                    shift(i, 0)
                    shift(i, 1)
                if nxt:
                    front(i.plus(1))
                if past:
                    turned(i.plus(-1), (0, 1))
                if now:
                    shift(i, 2)
                if past:
                    turned(i.plus(-1), (2,))
                if now:
                    shift(i, 3)
                if after:
                    norm_stats(i.plus(2))
                if out_of:
                    residual(i.plus(-2))
                if nxt:
                    front_k(i.plus(1))
                if past:
                    turned(i.plus(-1), (3, 4, 5))
                if now:
                    sums(i, 0)
                    sums(i, 1)
                if past:
                    attended(i.plus(-1))
                if after:
                    norm(i.plus(2))
                if now:
                    values(i)

            norm_stats(Step(0, 0))
            norm(Step(0, 0))
            split_weights()
            dve.wait_ge(w_zero, 5)
            dve.wait_ge(w_gain, 1)
            dve.wait_ge(w_bvwo, 1)
            V.tensor_tensor(bo_g[:], psT[:, 0, 0:D], bo_g[:], ALU.add).then_inc(w_bias, 1)
            dve.wait_ge(w_bias, 3)
            V.tensor_scalar(bo_g[:], bo_g[:], gains[:, 2:3], None, ALU.mult).then_inc(w_bias, 1)
            front(Step(0, 0))
            norm_stats(Step(0, 1))
            front_k(Step(0, 0))
            norm(Step(0, 1))
            for i in range(PEEL):
                iteration(Step(0, i))
            with dve.Fori(0, (B - 3 - PEEL) // 2) as k:
                iteration(Step(k, PEEL))
                iteration(Step(k, PEEL + 1))
            for i in range(B - 3, B + 2):
                iteration(Step(0, i))

            def stats2(p):
                dve.wait_ge(b_x[p.parity], p.loads())
                for t in range(TPP):
                    V.bn_stats(stats[:, t, :], x1p[:, p.parity, t, :]).then_inc(b_stat, 1)
                dve.wait_ge(b_stat, p.count(TPP, TPP))
                V.memset(gate[:, 1:2], 0.0)
                for t in range(TPP):
                    last = V.bn_aggr(mv[:, t, :], stats[:, t, :])
                last.then_inc(b_mv, 1)

            def norm2(p):
                dve.wait_ge(b_rstd, p.count(1, 1))
                dve.wait_ge(b_mv, p.count(1, 1))
                if p.has(2, 0):
                    dve.wait_ge(b_xTp, p.count(2, 0))
                for t in range(TPP):
                    last = V.tensor_scalar(xh2[:, t, :], x1p[:, p.parity, t, :], mv[:, t, 0:1], rstd[:, t:t + 1],
                                           ALU.subtract, ALU.mult)
                last.then_inc(b_xh, 1)

            def lo(p):
                for k in range(KD):
                    dve.wait_ge(b_xThi, p.count(2, k + 1))
                    V.tensor_tensor(x2T[:, p.parity, 1, k, :], psM[:, k, :], f32(x2T[:, p.parity, 0, k, :]),
                                    ALU.subtract).then_inc(b_xTlo, 1)

            def top2(p):
                dve.wait_ge(b_lgt, p.count(1, 1))
                V.tensor_copy(lg[:], psM[:, 1, 0:TPP * E].rearrange("p (t e) -> p t e", t=TPP)).then_inc(b_lg, 1)
                dve.wait_ge(b_lg, p.count(1, 1))
                V.memset(gate[:, 2:3], 0.0)
                for t in range(TPP):
                    last = V.max(top[:, t, :], lg[:, t, :])
                last.then_inc(b_top, 1)
                dve.wait_ge(b_top, p.count(1, 1))
                V.memset(gate[:, 3:4], 0.0)
                for t in range(TPP):
                    last = V.max_index(topi[:, t, :], top[:, t, :], lg[:, t, :])
                last.then_inc(b_topi, 1)
                V.tensor_tensor(ex[:], lg[:], top[:, :, 0:1].broadcast_to([P, TPP, E]), ALU.subtract
                                ).then_inc(b_sub, 1)
                dve.wait_ge(b_topi, p.count(1, 1))
                V.tensor_copy(topf[:], topi[:]).then_inc(b_topf, 1)
                dve.wait_ge(b_topf, p.count(1, 1))
                for n in range(2):
                    last = V.tensor_tensor(hot[:, n], iota[:].unsqueeze(1).broadcast_to([P, TPP, E]),
                                           topf[:, :, n:n + 1].broadcast_to([P, TPP, E]), ALU.is_equal)
                last.then_inc(b_hot, 1)

            def coefs(p):
                dve.wait_ge(b_exp, p.count(1, 1))
                V.tensor_reduce(esum[:], ex[:], AX.X, ALU.add).then_inc(b_sum, 1)
                dve.wait_ge(b_hot, p.count(1, 1))
                V.tensor_tensor(hot[:, 0], hot[:, 0], hot[:, 1], ALU.add).then_inc(b_sel, 1)
                dve.wait_ge(b_sum, p.count(1, 1))
                V.reciprocal(einv[:], esum[:]).then_inc(b_inv, 1)
                dve.wait_ge(b_sel, p.count(2, 1))
                V.tensor_tensor(ex[:], ex[:], hot[:, 0], ALU.mult).then_inc(b_sel, 1)
                dve.wait_ge(b_inv, p.count(1, 1))
                dve.wait_ge(b_sel, p.count(2, 2))
                V.tensor_tensor(ex[:], ex[:], einv[:].unsqueeze(2).broadcast_to([P, TPP, E]), ALU.mult
                                ).then_inc(b_cf, 1)
                dve.wait_ge(b_cf, p.count(2, 1))
                V.tensor_scalar(coef[:, p.parity], ex[:], gains[:, 3:4], None, ALU.mult).then_inc(b_cf, 1)

            def hidden(p, m):
                c = m % 2
                dve.wait_ge(b_sil, p.count(NCH, m + 1))
                dve.wait_ge(b_u, p.count(NCH, m + 1))
                if p.has(NCH, m - 1):
                    dve.wait_ge(b_hlo, p.count(NCH, m - 1))
                V.tensor_tensor(hf[:, c, :], psS[:, 2 * c + 1, :], sil[c], ALU.mult).then_inc(b_h, 1)
                dve.wait_ge(b_hhi, p.count(NCH, m + 1))
                V.tensor_tensor(h2[:, c, 1, :], hf[:, c, :], f32(h2[:, c, 0, :]), ALU.subtract
                                ).then_inc(b_hlo, 1)

            def add_up(p, m):
                if m == 0:
                    return
                dve.wait_ge(b_y, p.count(NCH, m + 1))
                if p.has(NCH - NSH + 1, m - 1):
                    dve.wait_ge(b_acc, p.count(NCH - NSH + 1, m - 1))
                if m == NSH - 1:
                    acc = x1p[:, p.parity].rearrange("p (a b) c -> p a (b c)", a=2)
                    last = V.scalar_tensor_tensor(acc, psT[:], gains[:, 3:4], acc, ALU.mult, ALU.add)
                else:
                    dve.wait_ge(b_cf, p.count(2, 2))
                    for t in range(TPP):
                        last = V.scalar_tensor_tensor(
                            x1p[:, p.parity, t, :], psT[:, t // 2, (t % 2) * D:(t % 2 + 1) * D],
                            coef[:, p.parity, t, m - NSH:m - NSH + 1], x1p[:, p.parity, t, :],
                            ALU.mult, ALU.add)
                last.then_inc(b_acc, 1)

            def pair(p, prep, nxt):
                for m in range(NCH):
                    if m + 1 < NCH:
                        hidden(p, m + 1)
                    elif nxt:
                        hidden(p.plus(1), 0)
                    add_up(p, m)
                    if prep and m == 1:
                        stats2(p.plus(1))
                    if prep and m == 2:
                        norm2(p.plus(1))
                    if prep and m == 3:
                        lo(p.plus(1))
                    if prep and m == 5:
                        top2(p.plus(1))
                    if prep and m == 7:
                        coefs(p.plus(1))

            stats2(Step(0, 0))
            norm2(Step(0, 0))
            lo(Step(0, 0))
            top2(Step(0, 0))
            coefs(Step(0, 0))
            hidden(Step(0, 0), 0)
            pair(Step(0, 0), True, True)
            with dve.Fori(0, (NPAIR - 2) // 2) as k:
                pair(Step(k, 1), True, True)
                pair(Step(k, 2), True, True)
            pair(Step(0, NPAIR - 1), False, False)

        @block.gpsimd
        def _(pool):
            G = nc.gpsimd

            def inv_std(step, n, mv_done, eps_done, rstd_done):
                pool.wait_ge(mv_done, step.count(1, 1))
                G.tensor_tensor(rstd[:, 0:n], mv[:, 0:n, 1], eps[:, 0:n], ALU.add).then_inc(eps_done, 1)
                pool.wait_ge(eps_done, step.count(1, 1))
                G.tensor_tensor(rstd[:, 0:n], rstd[:, 0:n], half_neg[:, 0:n], ALU.pow).then_inc(rstd_done, 1)

            def normalise(i, t):
                pool.wait_ge(a_rden, i.count(2, t + 1))
                for g2 in range(0, NG, 2):
                    v = pr[:, i.parity, t, g2:g2 + 2].rearrange("p g (k j) -> p g k j", j=HPG)
                    last = G.tensor_tensor(v, v, rden[:, t, HPG * g2:HPG * (g2 + 2)].rearrange("p (g j) -> p g j", g=2
                                           ).unsqueeze(2).broadcast_to([P, 2, LK, HPG]), ALU.mult)
                last.then_inc(a_pn, 1)

            def bias(b):
                pool.wait_ge(a_res[b.parity], b.loads())
                if b.has(1, 0):
                    pool.wait_ge(a_x1, b.count(1, 0))
                G.tensor_tensor(xbias[:], xres[:, b.parity], bo_g[:].unsqueeze(1).broadcast_to([P, TPB, D]),
                                ALU.add).then_inc(a_xb, 1)

            def front(b):
                pool.wait_ge(a_qhi, b.count(1, 1))
                if b.has(4, 0):
                    pool.wait_ge(a_s, b.count(4, 0))
                if b.has(1, -1):
                    pool.wait_ge(a_vlo, b.count(1, -1))
                if b.has(2, -2):
                    pool.wait_ge(a_pn, b.count(2, -2))
                for r in range(2):
                    rs, ro = slice(64 * r, 64 * r + 64), slice(64 * (1 - r), 64 * (1 - r) + 64)
                    G.tensor_tensor(qst[ro, r::2, :], qf[rs, :, :], f32(qst[rs, r::2, :]), ALU.subtract
                                    ).then_inc(a_qlo, 1)
                    pool.wait_ge(a_qlo, b.count(2, r + 1))
                pool.wait_ge(a_kthi, b.count(1, 1))
                G.tensor_tensor(kbd[:, 0].rearrange("p g k j -> p (g k) j"),
                                f32(kt2[:, 0]).rearrange("p g k -> p (g k)").unsqueeze(2).broadcast_to([P, NG * LK, HPG]),
                                mask[:, 0].unsqueeze(1).broadcast_to([P, NG * LK, HPG]), ALU.mult
                                ).then_inc(a_kbhi, 1)

            def attend(b):
                pool.wait_ge(a_ohi, b.count(1, 1))
                G.tensor_tensor(oT[:, 1], of[:], f32(oT[:, 0]), ALU.subtract).then_inc(a_olo, 1)

            def values(b):
                pool.wait_ge(a_vhi, b.count(1, 1))
                G.tensor_tensor(vbd[:, :, 1, :], vm[:].rearrange("p a j d -> p a (j d)"), f32(vbd[:, :, 0, :]),
                                ALU.subtract).then_inc(a_vlo, 1)

            def iteration(i):
                inner = not isinstance(i.k, int)
                now, nxt = inner or i.off < B, inner or i.off + 1 < B
                past, out_of = inner or 1 <= i.off <= B, inner or i.off >= 2
                if out_of:
                    attend(i.plus(-2))
                    bias(i.plus(-2))
                if past:
                    values(i.plus(-1))
                if nxt:
                    front(i.plus(1))
                if inner or i.off + 2 < B:
                    inv_std(i.plus(2), TPB, a_mv, a_eps, a_rstd)
                if now:
                    normalise(i, 0)
                    normalise(i, 1)

            pool.wait_ge(w_zero, 3)
            inv_std(Step(0, 0), TPB, a_mv, a_eps, a_rstd)
            front(Step(0, 0))
            inv_std(Step(0, 1), TPB, a_mv, a_eps, a_rstd)
            pool.wait_ge(w_bias, 4)
            for i in range(PEEL):
                iteration(Step(0, i))
            with pool.Fori(0, (B - 3 - PEEL) // 2) as k:
                iteration(Step(k, PEEL))
                iteration(Step(k, PEEL + 1))
            for i in range(B - 3, B + 2):
                iteration(Step(0, i))

            inv_std(Step(0, 0), TPP, b_mv, b_eps, b_rstd)
            inv_std(Step(0, 1), TPP, b_mv, b_eps, b_rstd)
            with pool.Fori(0, (NPAIR - 2) // 2) as k:
                inv_std(Step(k, 2), TPP, b_mv, b_eps, b_rstd)
                inv_std(Step(k, 3), TPP, b_mv, b_eps, b_rstd)




_INS = ['x', 'ctx_512', 'g_xattn', 'g_ffn', 'L0_xattn_Wq', 'L0_xattn_bq', 'L0_xattn_Wk', 'L0_xattn_bk',
        'L0_xattn_Wv', 'L0_xattn_bv', 'L0_xattn_Wo', 'L0_xattn_bo', 'L0_ffn_router', 'L0_ffn_experts_gate',
        'L0_ffn_experts_up', 'L0_ffn_experts_down', 'L0_ffn_shared_gate', 'L0_ffn_shared_up',
        'L0_ffn_shared_down']


def kernel(**inputs):
    import numpy as np
    import concourse.bacc as bacc
    from concourse.bass_utils import run_bass_kernel_spmd

    nc = bacc.Bacc("TRN2", target_bir_lowering=False, num_devices=1)
    arrays = {name: np.ascontiguousarray(inputs[name]) for name in _INS}
    arrays["ident"] = np.eye(P, dtype=np.float32)
    row = np.arange(P)[:, None]
    arrays["head_masks"] = np.stack([row % (HPG * DK) // DK == np.arange(HPG), row % HPG == np.arange(HPG)],
                                    1).astype(np.float32)
    arrays["expert_numbers"] = np.tile(np.arange(E, dtype=np.float32), (P, 1))
    args = [nc.dram_tensor("in_" + n, a.shape, mybir.dt.from_np(a.dtype), kind="ExternalInput").ap()
            for n, a in arrays.items()]
    out = nc.dram_tensor("out", (B * S, D), F32, kind="ExternalOutput").ap()
    build(nc, *args, out)
    r = run_bass_kernel_spmd(nc, [{"in_" + n: a for n, a in arrays.items()}], core_ids=[0])
    return r.results[0]["out"].reshape(B, S, D)
```

```python
from contextlib import ExitStack

import concourse.bass as bass
from concourse import mybir

F32 = mybir.dt.float32
F32R = mybir.dt.float32r
U32 = mybir.dt.uint32
ALU = mybir.AluOpType
ACT = mybir.ActivationFunctionType
AX = mybir.AxisListType

P = 128
B, S, D = 32, 256, 256
LK, DC = 77, 128
HEADS, DK = 16, 16
NG, HPG = 4, 4
GW = HPG * LK
LE = LK + LK % 2
NB = -(-GW // P)
REST = GW - (NB - 1) * P
TPB = S // P
KD = D // P
E, DE, DS = 8, 128, 256
NCH = DS // P + E
NSH = DS // P
FW = NCH * P
PAIR = 2 * S
TPP = PAIR // P
NPAIR = B * S // PAIR
EPS = 1e-5
PEEL = 5
FIRST, LAST = -3, B + 2
N_SMALL = 10
SCALE = DK ** -0.5
SHIFTED = 2


class Step:

    def __init__(self, k, off):
        self.k, self.off = k, off

    @property
    def index(self):
        return self.k * 2 + self.off

    @property
    def parity(self):
        return self.off % 2

    def plus(self, n):
        return Step(self.k, self.off + n)

    def count(self, per, n):
        return self.k * (2 * per) + (per * self.off + n)

    def has(self, per, n):
        assert isinstance(self.k, int) or per * self.off + n > 0, "a register may hold zero"
        return not isinstance(self.k, int) or self.count(per, n) > 0

    def exists(self):
        return self.has(1, 1)

    def loads(self, n=1):
        return self.k * (16 * n) + (self.off // 2 + 1) * (16 * n)


def live(i, off=0):
    return not isinstance(i.k, int) or 0 <= i.off + off < B


def f32(ap):
    return ap.bitcast(F32)


def build(nc, x, ctx_in, g_xattn, g_ffn, Wq, bq, Wk, bk, Wv, bv, Wo, bo, router,
          e_gate, e_up, e_down, s_gate, s_up, s_down, ident_in, mask_in, iota_in, out):
    with ExitStack() as ctx:
        def sb(name, shape, dt=F32):
            return ctx.enter_context(nc.sbuf_tensor(name, shape, dt))

        def sem(name):
            return ctx.enter_context(nc.semaphore(name))

        ident = sb("ident", [P, P])
        mask = sb("mask", [P, 2, HPG])
        iota = sb("iota", [P, E])
        gains = sb("gains", [P, 4])
        bq_c = sb("bq_c", [P, KD])
        bk_c = sb("bk_c", [P, NG])
        bv_c = sb("bv_c", [P, KD])
        bv_b = sb("bv_b", [P, 2, KD, P], F32R)
        bo_g = sb("bo_g", [P, D])
        half_neg = sb("half_neg", [P, TPP])
        eps = sb("eps", [P, TPP])
        gate = sb("gate", [P, 4])
        wq = sb("wq", [P, 2, KD, D], F32R)
        wk = sb("wk", [P, 2, NG, P], F32R)
        wv = sb("wv", [P, 2, D], F32R)
        wo = sb("wo", [P, 2, KD, D], F32R)
        wr = sb("wr", [P, 2, KD, P], F32R)
        wg = sb("wg", [P, 2, KD, FW], F32R)
        wu = sb("wu", [P, 2, KD, FW], F32R)
        wd = sb("wd", [P, 2, NCH, D], F32R)

        xin = sb("xin", [P, 2, TPB, D])
        cin = sb("cin", [LK, 2, DC])
        xres = sb("xres", [P, 2, TPB, D])
        xbias = sb("xbias", [P, TPB, D])
        x1b = sb("x1b", [P, 2, TPB, D])
        stats = sb("stats", [P, TPP, 6])
        mv = sb("mv", [P, TPP, 2])
        rstd = sb("rstd", [P, TPP])
        xh = sb("xh", [P, TPB, D])
        xT = sb("xT", [P, 2, KD, S], F32R)
        cT = sb("cT", [P, 2, 2, NB * P], F32R)
        qf = sb("qf", [P, KD, S])
        qst = sb("qst", [P, NG, S], F32R)
        kt = sb("kt", [P, NG, LK])
        kt2 = sb("kt2", [P, 2, NG, LK], F32R)
        kbd = sb("kbd", [P, 2, NG, LK, HPG], F32R)
        vm = sb("vm", [P, NB * NG, HPG, DK])
        vbd = sb("vbd", [P, NB * NG, 2, HPG * DK], F32R)
        pr = sb("pr", [P, 2, TPB, NG, GW])
        mx = sb("mx", [P, 4, HEADS // 2])
        den = sb("den", [P, TPB, HEADS])
        rden = sb("rden", [P, TPB, HEADS])
        pT = sb("pT", [P, 2, NB * NG, S], F32R)
        otmp = sb("otmp", [64, KD, 2 * S])
        of = sb("of", [P, KD, S])
        oT = sb("oT", [P, 2, KD, S], F32R)

        ffn_stage = sb("ffn_stage", [P, 3 * FW])
        sil = [qf[:].rearrange("p a b -> p (a b)"), of[:].rearrange("p a b -> p (a b)")]

        taken = [0]

        def over_pr(*dims):
            n = 1
            for d in dims:
                n *= d
            taken[0] += n
            flat = pr[:].rearrange("p a t g n -> p (a t g n)")[:, taken[0] - n:taken[0]]
            names = "abc"[:len(dims)]
            return flat.rearrange(f"p ({' '.join(names)}) -> p {' '.join(names)}", **dict(zip(names, dims))) \
                if len(dims) > 1 else flat

        x1p = over_pr(2, TPP, D)
        xh2 = over_pr(TPP, D)
        hf = over_pr(2, PAIR)
        lgT = over_pr(PAIR)[0:E]
        lg = over_pr(TPP, E)
        top = over_pr(TPP, 8)
        topi = over_pr(TPP, 8).bitcast(U32)
        topf = over_pr(TPP, 8)
        ex = over_pr(TPP, E)
        hot = over_pr(2, TPP, E)
        esum = over_pr(TPP)
        einv = over_pr(TPP)
        coef = over_pr(2, TPP, E)
        x2T = pT[:].rearrange("p a b c -> p (a b c)")[:, 4 * PAIR:12 * PAIR].rearrange(
            "p (a b c d) -> p a b c d", a=2, b=2, c=KD)
        h2 = pT[:].rearrange("p a b c -> p (a b c)")[:, 0:4 * PAIR].rearrange("p (a b c) -> p a b c", a=2, b=2)

        psS = ctx.enter_context(nc.psum_tensor("psS", [P, 4, 512], F32))
        psW = ctx.enter_context(nc.psum_tensor("psW", [P, 4, 512], F32))
        X_BANK, C_BANK, Q_BANK, K_BANK, V_BANK, O_BANK, Y_BANK = 1, 1, 3, 1, 2, 2, 0
        P_BANKS = (0, 1, 2, 0, 3, 2)
        psT, psM = psW[:, 0:2], psW[:, 2:4]

        x1_dram = nc.dram_tensor("x1_scratch", (B * S, D), F32, kind="Internal").ap()

        (w_in, w_hi, w_lo, w_zero, w_gain, w_bias, w_bvwo, w_bq) = map(sem, (
            "w_in", "w_hi", "w_lo", "w_zero", "w_gain", "w_bias", "w_bvwo", "w_bq"))
        w_stage = [sem(f"w_stage{n}") for n in range(8)]
        a_x = [sem("a_in0"), sem("a_in1")]
        a_res = [sem("a_res0"), sem("a_res1")]
        a_st = [sem("a_st0"), sem("a_st1")]
        (a_stat, a_mv, a_eps, a_rstd, a_xh, a_xTp, a_xThi, a_xTlo, a_cTp, a_cThi, a_cTlo, a_q, a_qf, a_qhi,
         a_qlo, a_k, a_kt, a_kthi, a_ktlo, a_kbhi, a_kblo, a_s, a_mx, a_sub, a_exp, a_den, a_rden, a_pn,
         a_pTp, a_pThi, a_pTlo, a_o, a_otmp, a_of, a_ohi, a_olo, a_v, a_vm, a_vhi, a_vlo, a_wo,
         a_xb, a_x1) = [sem("a_" + n) for n in (
            "stat mv eps rstd xh xTp xThi xTlo cTp cThi cTlo q qf qhi qlo k kt kthi ktlo kbhi kblo s mx "
            "sub exp den rden pn pTp pThi pTlo o otmp of ohi olo v vm vhi vlo wo xb x1").split()]
        b_x = [sem("b_x0"), sem("b_x1")]
        b_st = [sem("b_st0"), sem("b_st1")]
        (b_stat, b_mv, b_eps, b_rstd, b_xh, b_xTp, b_xThi, b_xTlo, b_lgp, b_lgT, b_lgt, b_lg, b_top, b_topi,
         b_topf, b_sub, b_exp, b_sum, b_inv, b_hot, b_sel, b_cf, b_g, b_u, b_sil, b_h, b_hhi, b_hlo, b_y,
         b_acc) = [sem("b_" + n) for n in (
            "stat mv eps rstd xh xTp xThi xTlo lgp lgT lgt lg top topi topf sub exp sum inv hot sel cf "
            "g u sil h hhi hlo y acc").split()]

        block = ctx.enter_context(nc.Block())

        rows = lambda w: w.rearrange("(k p) n -> p k n", p=P)
        one = lambda t, i: t[:, i].rearrange("p a b -> p (a b)") if len(t.shape) == 4 else t[:, i]
        jobs = [([(rows(Wq), 0, (KD, D))], lambda i: one(wq, i), KD * D),
                ([(Wk.rearrange("p (g n) -> p g n", g=NG), 64 * r, (NG, P, 64)) for r in range(2)],
                 lambda i: one(wk, i), NG * P),
                ([(Wv, 0, None)], lambda i: wv[:, i], D),
                ([(rows(Wo), 0, (KD, D))], lambda i: one(wo, i), KD * D),
                ([(rows(router), 0, (KD, E))], lambda i: wr[:, i, :, 0:E], KD * E)]
        for w_s, w_e, target in ((s_gate, e_gate, wg), (s_up, e_up, wu)):
            for k in range(KD):
                jobs.append(([(w_s[k * P:(k + 1) * P, :], 0, None),
                              (w_e[:, k * P:(k + 1) * P, :].rearrange("e p d -> p e d"), DS, (E, DE))],
                             lambda i, k=k, target=target: target[:, i, k, :], FW))
        for h in range(2):
            n0, n1 = (0, 5) if h == 0 else (5, NCH)
            parts = ([(rows(s_down), 0, (NSH, D))] if h == 0 else [])
            m0 = NSH if h == 0 else n0
            parts.append((e_down[m0 - NSH:n1 - NSH].rearrange("e p d -> p e d"), (m0 - n0) * D, (n1 - m0, D)))
            jobs.append((parts, lambda i, n0=n0, n1=n1: wd[:, i, n0:n1, :].rearrange("p a b -> p (a b)"),
                         (n1 - n0) * D))

        N_ATT = 5
        N_STAGE = 3
        att_at = [sum(job[2] for job in jobs[:n]) for n in range(N_ATT)]
        att_stage = pr[:, 0].rearrange("p t g n -> p (t g n)")

        def staged(n):
            width = jobs[n][2]
            if n < N_ATT:
                v = att_stage[:, att_at[n]:att_at[n] + width]
                return v.rearrange("p (a b) -> p a b", a=KD) if n == N_ATT - 1 else v
            at = (n - N_ATT) % N_STAGE * FW
            return ffn_stage[:, at:at + width]

        def stage_sem(n):
            return w_stage[n] if n < N_ATT else w_stage[N_ATT + (n - N_ATT) % N_STAGE]

        def ffn_job(i):
            return N_ATT + i - FIRST - 1

        def stage_count(n):
            same = [n] if n < N_ATT else range(N_ATT + (n - N_ATT) % N_STAGE, n + 1, N_STAGE)
            return 16 * sum(len(jobs[q][0]) for q in same)

        @block.sync
        def _(sp):
            def load_x(b):
                if b.has(1, -1):
                    sp.wait_ge(a_xh, b.count(1, -1))
                if b.has(1, -1):
                    sp.wait_ge(a_cTp, b.count(1, -1))
                sp.dma_start(xin[:, b.parity], x[b.index].rearrange("(t p) d -> p t d", p=P)
                             ).then_inc(a_x[b.parity], 16)
                sp.dma_start(cin[:, b.parity], ctx_in[b.index]).then_inc(a_x[b.parity], 16)

            def load_res(b):
                if b.has(1, -1):
                    sp.wait_ge(a_xb, b.count(1, -1))
                sp.dma_start(xres[:, b.parity], x[b.index].rearrange("(t p) d -> p t d", p=P)
                             ).then_inc(a_res[b.parity], 16)

            def store_x1(b):
                sp.wait_ge(a_x1, b.count(1, 1))
                sp.dma_start(x1_dram[bass.ds(b.index * S, S), :].rearrange("(t p) d -> p t d", p=P),
                             x1b[:, b.parity]).then_inc(a_st[b.parity], 16)

            def load_x1(p):
                if p.plus(-2).exists():
                    sp.wait_ge(b_st[p.plus(-2).parity], p.plus(-2).loads())
                sp.dma_start(x1p[:, p.parity],
                             x1_dram[bass.ds(p.index * PAIR, PAIR), :].rearrange("(t p) d -> p t d", p=P)
                             ).then_inc(b_x[p.parity], 16)

            def store_out(p):
                if p.has(NCH - NSH + 1, NCH - NSH + 1):
                    sp.wait_ge(b_acc, p.count(NCH - NSH + 1, NCH - NSH + 1))
                sp.dma_start(out[bass.ds(p.index * PAIR, PAIR), :].rearrange("(t p) d -> p t d", p=P),
                             x1p[:, p.parity]).then_inc(b_st[p.parity], 16)

            def load_weights(n):
                if n >= N_ATT + N_STAGE:
                    sp.wait_ge(w_lo, n - N_STAGE + 1)
                whole = staged(n) if n != N_ATT - 1 else att_stage[:, att_at[n]:att_at[n] + jobs[n][2]]
                for src, at, dims in jobs[n][0]:
                    if dims is None:
                        dst = whole[:, at:at + src.shape[1]]
                    elif len(dims) == 2:
                        dst = whole[:, at:at + dims[0] * dims[1]].rearrange("p (a b) -> p a b", a=dims[0])
                    else:
                        dst = whole[:, 0:dims[0] * dims[1]].rearrange("p (a b) -> p a b", a=dims[0])[
                            :, :, at:at + dims[2]]
                    sp.dma_start(dst, src).then_inc(stage_sem(n), 16)

            for n in range(N_ATT):
                load_weights(n)
            load_x(Step(0, 0))
            small = [(ident[:], ident_in), (mask[:], mask_in), (iota[:], iota_in),
                     (gains[:, 0:1], g_xattn.rearrange("(a b) -> a b", a=1).partition_broadcast(P)),
                     (gains[:, 1:2], g_ffn.rearrange("(a b) -> a b", a=1).partition_broadcast(P)),
                     (bq_c[:], bq.rearrange("(m p) -> p m", p=P)),
                     (bk_c[0:64, :], bk.rearrange("(g p) -> p g", p=64)),
                     (bk_c[64:P, :], bk.rearrange("(g p) -> p g", p=64)),
                     (bv_c[:], bv.rearrange("(m p) -> p m", p=P)),
                     (bo_g[:], bo.rearrange("(a b) -> a b", a=1).partition_broadcast(P))]
            for dst, src in small:
                sp.dma_start(dst, src, allow_slow_non_contiguous=True).then_inc(w_in, 16)
            load_x(Step(0, 1))
            for n in range(N_ATT, N_ATT + N_STAGE):
                load_weights(n)

            def iteration(i):
                if live(i, 3) and not (isinstance(i.k, int) and i.off + 3 < 2):
                    load_x(i.plus(3))
                if live(i, -1):
                    load_res(i.plus(-1))
                if live(i, -3):
                    store_x1(i.plus(-3))

            for i in range(FIRST, PEEL):
                iteration(Step(0, i))
                if N_ATT + N_STAGE <= ffn_job(i + 2) < len(jobs):
                    load_weights(ffn_job(i + 2))
            with sp.Fori(0, (B - 3 - PEEL) // 2) as k:
                iteration(Step(k, PEEL))
                iteration(Step(k, PEEL + 1))
            for i in range(B - 3, LAST):
                iteration(Step(0, i))
            sp.wait_ge(a_st[0], Step(0, 2).loads())
            sp.wait_ge(a_st[1], Step(0, 3).loads())
            sp.wait_ge(a_pTp, Step(0, B - 2).count(6, 6))
            load_x1(Step(0, 0))
            load_x1(Step(0, 1))
            iteration(Step(0, LAST))

            sp.wait_ge(a_st[Step(0, B - 2).parity], Step(0, B - 2).loads())
            sp.wait_ge(a_st[Step(0, B - 1).parity], Step(0, B - 1).loads())
            store_out(Step(0, 0))
            with sp.Fori(0, (NPAIR - 2) // 2) as k:
                for off in (1, 2):
                    load_x1(Step(k, off + 1))
                    store_out(Step(k, off))
            store_out(Step(0, NPAIR - 1))
            sp.wait_ge(b_st[Step(0, NPAIR - 2).parity], Step(0, NPAIR - 2).loads())
            sp.wait_ge(b_st[Step(0, NPAIR - 1).parity], Step(0, NPAIR - 1).loads())

        @block.tensor
        def _(pe):
            mm = nc.tensor.matmul

            def scores(b, s):
                t, hh = s // 2, s % 2
                if s == 0:
                    pe.wait_ge(a_qhi, b.count(1, 1))
                    pe.wait_ge(a_qlo, b.count(2, 2))
                    pe.wait_ge(a_kbhi, b.count(1, 1))
                    pe.wait_ge(a_kblo, b.count(1, 1))
                if s < 2:
                    if b.has(4, s - 1):
                        pe.wait_ge(a_exp, b.count(4, s - 1))
                else:
                    pe.wait_ge(a_sub, b.count(SHIFTED, s - 1))
                for g2 in range(2):
                    g = 2 * hh + g2
                    for part in range(2):
                        last = mm(psS[:, 2 * (s % 2) + g2, 0:GW], qst[:, g, t * P:(t + 1) * P],
                                  kbd[:, part, g].rearrange("p k j -> p (k j)"),
                                  start=(part == 0), stop=(part == 1))
                last.then_inc(a_s, 1)

            def out_proj(b):
                pe.wait_ge(a_ohi, b.count(1, 1))
                pe.wait_ge(a_olo, b.count(1, 1))
                for t in range(TPB):
                    n = 0
                    for m in range(KD):
                        for a, w in ((0, 0), (0, 1), (1, 0)):
                            last = mm(psW[:, Y_BANK, t * D:(t + 1) * D], oT[:, a, m, t * P:(t + 1) * P],
                                      wo[:, w, m, :], start=(n == 0), stop=(n == 5))
                            n += 1
                last.then_inc(a_wo, 1)

            def turn_x(b):
                pe.wait_ge(a_xh, b.count(1, 1))
                for k in range(KD):
                    for t in range(TPB):
                        last = nc.tensor.transpose(psW[:, X_BANK, k * S + t * P:k * S + (t + 1) * P],
                                                   xh[:, t, k * P:(k + 1) * P], ident[:])
                last.then_inc(a_xTp, 1)

            def turn_ctx(b):
                pe.wait_ge(a_x[b.parity], b.loads(2))
                nc.tensor.transpose(psW[:, C_BANK, 0:LK], cin[:, b.parity], ident[0:LK, 0:LK]).then_inc(a_cTp, 1)

            def queries(b):
                pe.wait_ge(a_xThi, b.count(1, 1))
                pe.wait_ge(a_xTlo, b.count(1, 1))
                for m in range(KD):
                    n = 0
                    for k in range(KD):
                        for w, a in ((0, 0), (1, 0), (0, 1)):
                            last = mm(psW[:, Q_BANK, m * S:(m + 1) * S], wq[:, w, k, m * P:(m + 1) * P],
                                      xT[:, a, k, :], start=(n == 0), stop=(n == 5))
                            n += 1
                last.then_inc(a_q, 1)

            def keys(b):
                pe.wait_ge(a_cThi, b.count(1, 1))
                pe.wait_ge(a_cTlo, b.count(1, 1))
                for g in range(NG):
                    for n, (w, a) in enumerate(((0, 0), (1, 0), (0, 1))):
                        last = mm(psW[:, K_BANK, g * LE:(g + 1) * LE], wk[:, w, g, :],
                                  cT[:, b.parity, a, 0:LE * HPG:HPG], start=(n == 0), stop=(n == 2))
                last.then_inc(a_k, 1)

            def values(b):
                pe.wait_ge(a_cThi, b.count(1, 1))
                pe.wait_ge(a_cTlo, b.count(1, 1))
                for blk in range(NB):
                    for n, (a, w) in enumerate(((0, 0), (0, 1), (1, 0))):
                        last = mm(psW[:, V_BANK + blk // 2, (blk % 2) * D:(blk % 2 + 1) * D],
                                  cT[:, b.parity, a, blk * P:(blk + 1) * P], wv[:, w, :], start=(n == 0), stop=(n == 2))
                last.then_inc(a_v, 1)

            def turn_p(b, s):
                t, blk = s // NB, s % NB
                pe.wait_ge(a_pn, b.count(2, t + 1))
                flat = pr[:, b.parity, t].rearrange("p g n -> p (g n)")
                for g in range(NG):
                    rows_of = P if blk < NB - 1 or g == 0 else REST
                    at = g * GW + blk * P
                    last = nc.tensor.transpose(psW[0:rows_of, P_BANKS[s], g * P:(g + 1) * P],
                                               flat[:, at:at + rows_of], ident[:])
                last.then_inc(a_pTp, 1)

            def attend(b):
                pe.wait_ge(a_pThi, b.count(6, 6))
                pe.wait_ge(a_pTlo, b.count(6, 6))
                pe.wait_ge(a_vhi, b.count(1, 1))
                pe.wait_ge(a_vlo, b.count(1, 1))
                for g in range(NG):
                    n = 0
                    for blk in range(NB):
                        for part in range(2):
                            last = mm(psW[:, O_BANK + g // 2, (g % 2) * S:(g % 2 + 1) * S],
                                      vbd[:, blk * NG + g].rearrange("p a b -> p (a b)"),
                                      pT[:, part, blk * NG + g, :], start=(n == 0), stop=(n == 2 * NB - 1))
                            n += 1
                last.then_inc(a_o, 1)

            def iteration(i):
                if live(i, 1):
                    if live(i, -1):
                        pe.wait_ge(a_pTlo, i.plus(-1).count(6, 2))
                    else:
                        pe.wait_ge(a_xTlo, i.plus(1).count(1, 1))
                    turn_ctx(i.plus(1))
                if live(i, -1):
                    pe.wait_ge(a_pTlo, i.plus(-1).count(6, 1))
                    turn_p(i.plus(-1), 3)
                if live(i, -1):
                    if live(i, 1):
                        pe.wait_ge(a_qf, i.plus(1).count(1, 1))
                    else:
                        pe.wait_ge(a_vm, i.plus(-1).count(1, 1))
                    turn_p(i.plus(-1), 4)
                if live(i, 1):
                    pe.wait_ge(a_cTlo, i.plus(1).count(1, 1))
                    keys(i.plus(1))
                if live(i, -1):
                    pe.wait_ge(a_pTlo, i.plus(-1).count(6, 3))
                    turn_p(i.plus(-1), 5)
                if live(i, -2):
                    if live(i, -1):
                        pe.wait_ge(a_pTlo, i.plus(-1).count(6, 4))
                    elif live(i, -3):
                        pe.wait_ge(a_x1, i.plus(-3).count(1, 1))
                    out_proj(i.plus(-2))
                if live(i, -1):
                    pe.wait_ge(a_pTlo, i.plus(-1).count(6, 6))
                    pe.wait_ge(a_pTlo, i.plus(-1).count(6, 5))
                    attend(i.plus(-1))
                if live(i, 2):
                    if live(i, 1):
                        pe.wait_ge(a_kt, i.plus(1).count(1, 1))
                    elif live(i, -1):
                        pe.wait_ge(a_pTlo, i.plus(-1).count(6, 2))
                    turn_x(i.plus(2))
                if live(i, 1):
                    scores(i.plus(1), 0)
                if live(i):
                    if live(i, -1):
                        pe.wait_ge(a_of, i.plus(-1).count(1, 1))
                    if live(i, -1):
                        pe.wait_ge(a_of, i.plus(-1).count(1, 1))
                    elif live(i, 1):
                        pe.wait_ge(a_qf, i.plus(1).count(1, 1))
                    values(i)
                if live(i):
                    if live(i, -2):
                        pe.wait_ge(a_x1, i.plus(-2).count(1, 1))
                    elif live(i, -1):
                        pe.wait_ge(a_pTlo, i.plus(-1).count(6, 4))
                    turn_p(i, 0)
                if live(i, 1):
                    scores(i.plus(1), 1)
                    scores(i.plus(1), 2)
                if live(i):
                    if live(i, 2):
                        pe.wait_ge(a_xTlo, i.plus(2).count(1, 1))
                    elif live(i, 1):
                        pe.wait_ge(a_kt, i.plus(1).count(1, 1))
                    elif live(i, -1):
                        pe.wait_ge(a_pTlo, i.plus(-1).count(6, 2))
                    turn_p(i, 1)
                if live(i):
                    pe.wait_ge(a_vm, i.count(1, 1))
                    turn_p(i, 2)
                if live(i, 2):
                    if live(i):
                        pe.wait_ge(a_vm, i.count(1, 1))
                    elif live(i, -1):
                        pe.wait_ge(a_of, i.plus(-1).count(1, 1))
                    elif live(i, 1):
                        pe.wait_ge(a_qf, i.plus(1).count(1, 1))
                    queries(i.plus(2))
                if live(i, 1):
                    scores(i.plus(1), 3)

            pe.wait_ge(w_lo, 2)
            pe.wait_ge(w_hi, 2)
            pe.wait_ge(w_in, 16 * N_SMALL)
            pe.wait_ge(w_lo, N_ATT)
            pe.wait_ge(w_bias, 2)
            n = 0
            for m in range(KD):
                for a, w in ((0, 0), (0, 1), (1, 0)):
                    last = mm(psT[:, 0, 0:D], bv_b[:, a, m, :], wo[:, w, m, :], start=(n == 0), stop=(n == 5))
                    n += 1
            last.then_inc(w_bvwo, 1)
            pe.wait_ge(w_bias, 3)
            for i in range(FIRST, PEEL):
                iteration(Step(0, i))
            with pe.Fori(0, (B - 3 - PEEL) // 2) as k:
                iteration(Step(k, PEEL))
                iteration(Step(k, PEEL + 1))
            for i in range(B - 3, LAST + 1):
                iteration(Step(0, i))

            def transposes(p):
                pe.wait_ge(b_xh, p.count(1, 1))
                if p.has(1, 0):
                    pe.wait_ge(b_lg, p.count(1, 0))
                for k in range(KD):
                    for t in range(TPP):
                        last = nc.tensor.transpose(psM[:, k, t * P:(t + 1) * P],
                                                   xh2[:, t, k * P:(k + 1) * P], ident[:])
                    last.then_inc(b_xTp, 1)

            def route(p):
                pe.wait_ge(b_xThi, p.count(2, 2))
                pe.wait_ge(b_xTlo, p.count(2, 2))
                n = 0
                for k in range(KD):
                    for w, a in ((0, 0), (1, 0), (0, 1)):
                        last = mm(psM[:, 0, :], wr[:, w, k, :], x2T[:, p.parity, a, k, :],
                                  start=(n == 0), stop=(n == 5))
                        n += 1
                last.then_inc(b_lgp, 1)

            def route_back(p):
                if isinstance(p.k, int):
                    pe.wait_ge(b_lgT, p.count(1, 1))
                for t in range(TPP):
                    last = nc.tensor.transpose(psM[:, 1, t * E:(t + 1) * E], lgT[:, t * P:(t + 1) * P],
                                               ident[0:E, 0:E])
                last.then_inc(b_lgt, 1)

            def gate_up(p, m):
                c = m % 2
                if p.has(NCH, m - 1):
                    pe.wait_ge(b_h, p.count(NCH, m - 1))
                for w2, base, done in ((wg, 0, b_g), (wu, 1, b_u)):
                    n = 0
                    for k in range(KD):
                        for w, a in ((0, 0), (1, 0), (0, 1)):
                            last = mm(psS[:, 2 * c + base, :], w2[:, w, k, m * P:(m + 1) * P],
                                      x2T[:, p.parity, a, k, :], start=(n == 0), stop=(n == 5))
                            n += 1
                    last.then_inc(done, 1)

            def down(p, m, ahead=False):
                c = m % 2
                pe.wait_ge(b_hhi, p.count(NCH, m + 1))
                pe.wait_ge(b_hlo, p.count(NCH, m + 1))
                if m != 1:
                    if p.has(NCH - NSH + 1, max(m - 1, 0)):
                        pe.wait_ge(b_acc, p.count(NCH - NSH + 1, max(m - 1, 0)))
                for t in range(TPP):
                    if ahead and t == TPP - 1:
                        pe.wait_ge(b_lgT, p.plus(1).count(1, 1))
                    for n, (a, w) in enumerate(((0, 0), (0, 1), (1, 0))):
                        if m < NSH:
                            start = m == 0 and n == 0 and t % 2 == 0
                            stop = m == NSH - 1 and n == 2
                        else:
                            start, stop = n == 0, n == 2
                        last = mm(psT[:, t // 2, (t % 2) * D:(t % 2 + 1) * D],
                                  h2[:, c, a, t * P:(t + 1) * P], wd[:, w, m, :],
                                  start=start, stop=stop, skip_group_check=(m < NSH))
                last.then_inc(b_y, 1)

            def pair(p, prep, nxt):
                for m in range(NCH):
                    if m + 1 < NCH:
                        gate_up(p, m + 1)
                    elif nxt:
                        gate_up(p.plus(1), 0)
                    if m > 0:
                        down(p, m - 1, prep and m == 6)
                    elif not isinstance(p.k, int) or p.off > 0:
                        down(p.plus(-1), NCH - 1)
                    if prep and m == 4:
                        transposes(p.plus(1))
                    if prep and m == 5:
                        route(p.plus(1))
                    if prep and m == 6:
                        route_back(p.plus(1))

            pe.wait_ge(w_lo, len(jobs))
            transposes(Step(0, 0))
            route(Step(0, 0))
            route_back(Step(0, 0))
            gate_up(Step(0, 0), 0)
            pair(Step(0, 0), True, True)
            with pe.Fori(0, (NPAIR - 2) // 2) as k:
                pair(Step(k, 1), True, True)
                pair(Step(k, 2), True, True)
            pair(Step(0, NPAIR - 1), False, False)
            down(Step(0, NPAIR - 1), NCH - 1)

        @block.scalar
        def _(act):
            def split_hi(n):
                act.wait_ge(stage_sem(n), stage_count(n))
                if n == N_ATT - 1:
                    act.wait_ge(w_zero, 1)
                nc.scalar.copy(jobs[n][1](0), staged(n)).then_inc(w_hi, 1)

            for n in range(N_ATT):
                split_hi(n)
            act.wait_ge(w_in, 16 * N_SMALL)
            nc.scalar.activation(gains[:, 2:4], gains[:, 0:2], ACT.Tanh).then_inc(w_gain, 1)

            def x_hi(b):
                act.wait_ge(a_xTp, b.count(1, 1))
                if b.has(1, 0):
                    act.wait_ge(a_q, b.count(1, 0))
                nc.scalar.copy(xT[:, 0].rearrange("p a b -> p (a b)"), psW[:, X_BANK, :]).then_inc(a_xThi, 1)

            def ctx_hi(b):
                act.wait_ge(a_cTp, b.count(1, 1))
                if b.has(1, -1):
                    act.wait_ge(a_v, b.count(1, -1))
                if b.has(1, -1):
                    act.wait_ge(a_k, b.count(1, -1))
                nc.scalar.copy(cT[:, b.parity, 0, 0:GW].rearrange("p (k j) -> p k j", j=HPG),
                               psW[:, C_BANK, 0:LK].unsqueeze(2).broadcast_to([P, LK, HPG])).then_inc(a_cThi, 1)

            def queries_out(b):
                act.wait_ge(a_q, b.count(1, 1))
                if b.has(2, 0):
                    act.wait_ge(a_qlo, b.count(2, 0))
                for m in range(KD):
                    last = nc.scalar.activation(qf[:, m, :], psW[:, Q_BANK, m * S:(m + 1) * S], ACT.Identity,
                                                bias=bq_c[:, m:m + 1], scale=SCALE)
                last.then_inc(a_qf, 1)

            def queries_hi(b):
                if b.has(4, 0):
                    act.wait_ge(a_s, b.count(4, 0))
                act.wait_ge(a_qf, b.count(1, 1))
                for r in range(2):
                    rs = slice(64 * r, 64 * r + 64)
                    last = nc.scalar.copy(qst[rs, r::2, :], qf[rs, :, :])
                last.then_inc(a_qhi, 1)

            def keys_hi(b):
                act.wait_ge(a_kt, b.count(1, 1))
                if b.has(1, 0):
                    act.wait_ge(a_kbhi, b.count(1, 0))
                nc.scalar.copy(kt2[:, 0], kt[:]).then_inc(a_kthi, 1)

            def keys_spread_lo(b):
                act.wait_ge(a_ktlo, b.count(1, 1))
                if b.has(4, 0):
                    act.wait_ge(a_s, b.count(4, 0))
                for j in range(HPG):
                    last = nc.scalar.activation(kbd[:, 1, :, :, j], f32(kt2[:, 1]), ACT.Copy,
                                                scale=mask[:, 0, j:j + 1])
                last.then_inc(a_kblo, 1)

            def exps(b, s):
                t, hh = s // 2, s % 2
                if s < SHIFTED:
                    act.wait_ge(a_sub, b.count(SHIFTED, s + 1))
                    v = pr[:, b.parity, t, 2 * hh:2 * hh + 2, :]
                    last = nc.scalar.activation(v, v, ACT.Exp)
                else:
                    act.wait_ge(a_mx, b.count(4, s + 1))
                    for g2 in range(2):
                        for j in range(HPG):
                            last = nc.scalar.activation(pr[:, b.parity, t, 2 * hh + g2, j::HPG],
                                                        psS[:, 2 * (s % 2) + g2, j:GW:HPG], ACT.Exp,
                                                        bias=mx[:, s, g2 * HPG + j:g2 * HPG + j + 1])
                last.then_inc(a_exp, 1)

            def turned_hi(b, s):
                t, blk = s // NB, s % NB
                rs = slice(0, P if blk < NB - 1 else REST)
                act.wait_ge(a_pTp, b.count(6, s + 1))
                if s == 0:
                    if b.has(1, 0):
                        act.wait_ge(a_o, b.count(1, 0))
                nc.scalar.copy(pT[rs, 0, NG * blk:NG * (blk + 1), t * P:(t + 1) * P],
                               psW[rs, P_BANKS[s]].rearrange("p (g n) -> p g n", g=NG)).then_inc(a_pThi, 1)

            def attended(b):
                act.wait_ge(a_o, b.count(1, 1))
                if b.has(1, 0):
                    act.wait_ge(a_of, b.count(1, 0))
                nc.scalar.copy(otmp[:], psW[64:P, O_BANK:O_BANK + 2, :]).then_inc(a_otmp, 1)

            def attended_hi(b):
                act.wait_ge(a_of, b.count(1, 1))
                if b.has(1, 0):
                    act.wait_ge(a_wo, b.count(1, 0))
                nc.scalar.copy(oT[:, 0], of[:]).then_inc(a_ohi, 1)

            def values_own(b):
                act.wait_ge(a_v, b.count(1, 1))
                if b.has(1, 0):
                    act.wait_ge(a_vlo, b.count(1, 0))
                rows_v = psW[:, V_BANK:V_BANK + 2, :].rearrange("p a b -> p (a b)")[:, 0:NB * D].rearrange(
                    "p (a j d) -> p a j d", j=HPG, d=DK)
                for j in range(HPG):
                    last = nc.scalar.activation(vm[:, :, j, :], rows_v[:, :, j, :], ACT.Copy,
                                                scale=mask[:, 1, j:j + 1])
                last.then_inc(a_vm, 1)

            def values_hi(b):
                act.wait_ge(a_vm, b.count(1, 1))
                if b.has(1, 0):
                    act.wait_ge(a_o, b.count(1, 0))
                nc.scalar.copy(vbd[:, :, 0, :], vm[:].rearrange("p a j d -> p a (j d)")).then_inc(a_vhi, 1)

            def iteration(i):
                if live(i, 1):
                    queries_out(i.plus(1))
                    ctx_hi(i.plus(1))
                if live(i, -1):
                    turned_hi(i.plus(-1), 2)
                    turned_hi(i.plus(-1), 3)
                    turned_hi(i.plus(-1), 4)
                if live(i, 1):
                    queries_hi(i.plus(1))
                if live(i):
                    exps(i, 1)
                if live(i, -1):
                    turned_hi(i.plus(-1), 5)
                if live(i, 1):
                    keys_hi(i.plus(1))
                if live(i):
                    exps(i, 2)
                if live(i, 1):
                    keys_spread_lo(i.plus(1))
                if live(i, -1):
                    attended(i.plus(-1))
                if live(i):
                    exps(i, 3)
                if live(i, -1):
                    attended_hi(i.plus(-1))
                if live(i, 2):
                    x_hi(i.plus(2))
                if live(i, 1):
                    exps(i.plus(1), 0)
                if live(i):
                    turned_hi(i, 0)
                    values_own(i)
                    turned_hi(i, 1)
                    values_hi(i)

            act.wait_ge(w_zero, 5)
            act.wait_ge(w_bq, 1)
            for i in range(FIRST, PEEL):
                if N_ATT <= ffn_job(i) < len(jobs):
                    split_hi(ffn_job(i))
                iteration(Step(0, i))
            with act.Fori(0, (B - 3 - PEEL) // 2) as k:
                iteration(Step(k, PEEL))
                iteration(Step(k, PEEL + 1))
            for i in range(B - 3, LAST + 1):
                iteration(Step(0, i))

            def hi(p):
                for k in range(KD):
                    act.wait_ge(b_xTp, p.count(2, k + 1))
                    nc.scalar.copy(x2T[:, p.parity, 0, k, :], psM[:, k, :]).then_inc(b_xThi, 1)

            def logits(p):
                act.wait_ge(b_lgp, p.count(1, 1))
                if p.has(1, 0):
                    act.wait_ge(b_lgt, p.count(1, 0))
                nc.scalar.copy(lgT[:], psM[0:E, 0, :]).then_inc(b_lgT, 1)

            def exp(p):
                act.wait_ge(b_sub, p.count(1, 1))
                nc.scalar.activation(ex[:], ex[:], ACT.Exp).then_inc(b_exp, 1)

            def chunk(p, m):
                act.wait_ge(b_g, p.count(NCH, m + 1))
                if p.has(NCH, m - 1):
                    act.wait_ge(b_h, p.count(NCH, m - 1))
                nc.scalar.activation(sil[m % 2], psS[:, 2 * (m % 2), :], ACT.Silu).then_inc(b_sil, 1)
                act.wait_ge(b_h, p.count(NCH, m + 1))
                if p.has(NCH, m - 1):
                    act.wait_ge(b_y, p.count(NCH, m - 1))
                nc.scalar.copy(h2[:, m % 2, 0, :], hf[:, m % 2, :]).then_inc(b_hhi, 1)

            def pair(p, prep):
                for m in range(NCH):
                    chunk(p, m)
                    if prep and m == 5:
                        hi(p.plus(1))
                    if prep and m == 6:
                        logits(p.plus(1))
                    if prep and m == 8:
                        exp(p.plus(1))

            hi(Step(0, 0))
            logits(Step(0, 0))
            exp(Step(0, 0))
            pair(Step(0, 0), True)
            with act.Fori(0, (NPAIR - 2) // 2) as k:
                pair(Step(k, 1), True)
                pair(Step(k, 2), True)
            pair(Step(0, NPAIR - 1), False)

        @block.vector
        def _(dve):
            V = nc.vector
            V.memset(f32(wr[:]), 0.0).then_inc(w_zero, 1)
            V.memset(eps[:], EPS).then_inc(w_zero, 1)
            V.memset(half_neg[:], -0.5).then_inc(w_zero, 1)

            def stats_of(b, src, done):
                for t in range(TPB):
                    V.bn_stats(stats[:, t, :], src[:, t, :]).then_inc(a_stat, 1)
                dve.wait_ge(a_stat, b.count(TPB, TPB))
                V.memset(gate[:, 0:1], 0.0)
                for t in range(TPB):
                    last = V.bn_aggr(mv[:, t, :], stats[:, t, :])
                last.then_inc(done, 1)

            def norm_stats(b):
                dve.wait_ge(a_x[b.parity], b.loads(2))
                stats_of(b, xin[:, b.parity], a_mv)

            def norm(b):
                dve.wait_ge(a_rstd, b.count(1, 1))
                dve.wait_ge(a_mv, b.count(1, 1))
                if b.has(1, 0):
                    dve.wait_ge(a_xTp, b.count(1, 0))
                for t in range(TPB):
                    last = V.tensor_scalar(xh[:, t, :], xin[:, b.parity, t, :], mv[:, t, 0:1], rstd[:, t:t + 1],
                                           ALU.subtract, ALU.mult)
                last.then_inc(a_xh, 1)

            def split_lo(n):
                dve.wait_ge(w_hi, n + 1)
                V.tensor_tensor(jobs[n][1](1), staged(n), f32(jobs[n][1](0)), ALU.subtract).then_inc(w_lo, 1)

            def maxima(b, s):
                t, hh = s // 2, s % 2
                dve.wait_ge(a_s, b.count(4, s + 1))
                if s >= SHIFTED:
                    if b.has(4, s - 3):
                        dve.wait_ge(a_exp, b.count(4, s - 3))
                elif b.has(SHIFTED, s - SHIFTED + 1):
                    dve.wait_ge(a_sub, b.count(SHIFTED, s - SHIFTED + 1))
                bank = psS[:, 2 * (s % 2):2 * (s % 2) + 2, 0:GW]
                V.tensor_reduce(mx[:, s, :], bank.rearrange("p g (k j) -> p g j k", j=HPG), AX.X, ALU.max,
                                negate=(s >= SHIFTED)).then_inc(a_mx, 1)
                if s < SHIFTED:
                    dve.wait_ge(a_mx, b.count(4, s + 1))
                    if s == 0:
                        if b.has(6, -6):
                            dve.wait_ge(a_pTp, b.count(6, -6))
                    V.tensor_tensor(
                        pr[:, b.parity, t, 2 * hh:2 * hh + 2, :].rearrange("p g (k j) -> p g k j", j=HPG),
                        bank.rearrange("p g (k j) -> p g k j", j=HPG),
                        mx[:, s, :].rearrange("p (g j) -> p g j", g=2).unsqueeze(2).broadcast_to([P, 2, LK, HPG]),
                        ALU.subtract).then_inc(a_sub, 1)

            def sums(b, t):
                dve.wait_ge(a_exp, b.count(4, 2 * t + 2))
                if b.has(2, t - 1):
                    dve.wait_ge(a_rden, b.count(2, t - 1))
                V.tensor_reduce(den[:, t, :], pr[:, b.parity, t].rearrange("p g (k j) -> p g j k", j=HPG),
                                AX.X, ALU.add).then_inc(a_den, 1)
                dve.wait_ge(a_den, b.count(2, t + 1))
                if b.has(2, t - 1):
                    dve.wait_ge(a_pn, b.count(2, t - 1))
                V.reciprocal(rden[:, t, :], den[:, t, :]).then_inc(a_rden, 1)

            def residual(b):
                dve.wait_ge(a_wo, b.count(1, 1))
                dve.wait_ge(a_xb, b.count(1, 1))
                if b.plus(-2).exists():
                    dve.wait_ge(a_st[b.parity], b.plus(-2).loads())
                V.scalar_tensor_tensor(x1b[:, b.parity].rearrange("p a b -> p (a b)"), psW[:, Y_BANK, :],
                                       gains[:, 2:3], xbias[:].rearrange("p a b -> p (a b)"),
                                       ALU.mult, ALU.add).then_inc(a_x1, 1)

            def x_lo(b):
                dve.wait_ge(a_xThi, b.count(1, 1))
                V.tensor_tensor(xT[:, 1].rearrange("p a b -> p (a b)"), psW[:, X_BANK, :],
                                f32(xT[:, 0]).rearrange("p a b -> p (a b)"), ALU.subtract).then_inc(a_xTlo, 1)

            def ctx_lo(b):
                dve.wait_ge(a_cThi, b.count(1, 1))
                V.tensor_tensor(cT[:, b.parity, 1, 0:GW].rearrange("p (k j) -> p k j", j=HPG),
                                psW[:, C_BANK, 0:LK].unsqueeze(2).broadcast_to([P, LK, HPG]),
                                f32(cT[:, b.parity, 0, 0:GW]).rearrange("p (k j) -> p k j", j=HPG), ALU.subtract
                                ).then_inc(a_cTlo, 1)

            def keys_out(b):
                dve.wait_ge(a_k, b.count(1, 1))
                if b.has(1, 0):
                    dve.wait_ge(a_kthi, b.count(1, 0))
                if b.has(1, 0):
                    dve.wait_ge(a_ktlo, b.count(1, 0))
                V.tensor_tensor(kt[:], psW[:, K_BANK, 0:NG * LE].rearrange("p (g k) -> p g k", g=NG)[:, :, 0:LK],
                                bk_c[:].unsqueeze(2).broadcast_to([P, NG, LK]), ALU.add).then_inc(a_kt, 1)

            def keys_lo(b):
                dve.wait_ge(a_kthi, b.count(1, 1))
                dve.wait_ge(a_kt, b.count(1, 1))
                if b.has(1, 0):
                    dve.wait_ge(a_kblo, b.count(1, 0))
                V.tensor_tensor(kt2[:, 1], kt[:], f32(kt2[:, 0]), ALU.subtract).then_inc(a_ktlo, 1)

            def turned_lo(b, s):
                t, blk = s // NB, s % NB
                rs = slice(0, P if blk < NB - 1 else REST)
                dve.wait_ge(a_pThi, b.count(6, s + 1))
                V.tensor_tensor(pT[rs, 1, NG * blk:NG * (blk + 1), t * P:(t + 1) * P],
                                psW[rs, P_BANKS[s]].rearrange("p (g n) -> p g n", g=NG),
                                f32(pT[rs, 0, NG * blk:NG * (blk + 1), t * P:(t + 1) * P]), ALU.subtract
                                ).then_inc(a_pTlo, 1)

            def attended(b):
                dve.wait_ge(a_otmp, b.count(1, 1))
                if b.has(1, 0):
                    dve.wait_ge(a_ohi, b.count(1, 0))
                if b.has(1, 0):
                    dve.wait_ge(a_olo, b.count(1, 0))
                for r in range(2):
                    last = V.tensor_tensor(of[64 * r:64 * r + 64, :, :], psW[0:64, O_BANK:O_BANK + 2, r * S:(r + 1) * S],
                                           otmp[:, :, r * S:(r + 1) * S], ALU.add)
                last.then_inc(a_of, 1)

            def iteration(i):
                if live(i, -1):
                    maxima(i.plus(-1), 2)
                if live(i):
                    ctx_lo(i)
                if live(i, -2):
                    turned_lo(i.plus(-2), 2)
                    turned_lo(i.plus(-2), 3)
                    turned_lo(i.plus(-2), 4)
                if live(i):
                    keys_out(i)
                if live(i, -1):
                    maxima(i.plus(-1), 3)
                if live(i, -2):
                    turned_lo(i.plus(-2), 5)
                if live(i, -3):
                    residual(i.plus(-3))
                if live(i):
                    keys_lo(i)
                if live(i, -1):
                    sums(i.plus(-1), 0)
                if live(i, 2):
                    norm_stats(i.plus(2))
                if live(i, -2):
                    attended(i.plus(-2))
                if live(i):
                    maxima(i, 0)
                if live(i, 1):
                    x_lo(i.plus(1))
                if live(i, -1):
                    sums(i.plus(-1), 1)
                if live(i):
                    maxima(i, 1)
                if live(i, -1):
                    turned_lo(i.plus(-1), 0)
                    turned_lo(i.plus(-1), 1)
                if live(i, 2):
                    norm(i.plus(2))

            for n in range(N_ATT):
                split_lo(n)
            V.memset(f32(pT[:, :, NG * (NB - 1):, :]), 0.0).then_inc(w_zero, 1)
            V.memset(f32(cT[:, :, :, GW:]), 0.0).then_inc(w_zero, 1)
            dve.wait_ge(w_in, 16 * N_SMALL)
            V.tensor_scalar(bq_c[:], bq_c[:], SCALE, None, ALU.mult).then_inc(w_bq, 1)
            bv_cols = bv_c[:].unsqueeze(2).broadcast_to([P, KD, P])
            V.tensor_copy(bv_b[:, 0], bv_cols).then_inc(w_bias, 1)
            dve.wait_ge(w_bias, 1)
            V.tensor_tensor(bv_b[:, 1], bv_cols, f32(bv_b[:, 0]), ALU.subtract).then_inc(w_bias, 1)
            dve.wait_ge(w_lo, N_ATT)
            dve.wait_ge(w_zero, 5)
            dve.wait_ge(w_gain, 1)
            dve.wait_ge(w_bvwo, 1)
            V.tensor_tensor(bo_g[:], psT[:, 0, 0:D], bo_g[:], ALU.add).then_inc(w_bias, 1)
            dve.wait_ge(w_bias, 3)
            V.tensor_scalar(bo_g[:], bo_g[:], gains[:, 2:3], None, ALU.mult).then_inc(w_bias, 1)
            for i in range(FIRST, PEEL):
                iteration(Step(0, i))
                if N_ATT <= ffn_job(i) < len(jobs):
                    split_lo(ffn_job(i))
            with dve.Fori(0, (B - 3 - PEEL) // 2) as k:
                iteration(Step(k, PEEL))
                iteration(Step(k, PEEL + 1))
            for i in range(B - 3, LAST + 1):
                iteration(Step(0, i))

            def stats2(p):
                dve.wait_ge(b_x[p.parity], p.loads())
                for t in range(TPP):
                    V.bn_stats(stats[:, t, :], x1p[:, p.parity, t, :]).then_inc(b_stat, 1)
                dve.wait_ge(b_stat, p.count(TPP, TPP))
                V.memset(gate[:, 1:2], 0.0)
                for t in range(TPP):
                    last = V.bn_aggr(mv[:, t, :], stats[:, t, :])
                last.then_inc(b_mv, 1)

            def norm2(p):
                dve.wait_ge(b_rstd, p.count(1, 1))
                dve.wait_ge(b_mv, p.count(1, 1))
                if p.has(2, 0):
                    dve.wait_ge(b_xTp, p.count(2, 0))
                for t in range(TPP):
                    last = V.tensor_scalar(xh2[:, t, :], x1p[:, p.parity, t, :], mv[:, t, 0:1], rstd[:, t:t + 1],
                                           ALU.subtract, ALU.mult)
                last.then_inc(b_xh, 1)

            def lo(p):
                for k in range(KD):
                    dve.wait_ge(b_xThi, p.count(2, k + 1))
                    V.tensor_tensor(x2T[:, p.parity, 1, k, :], psM[:, k, :], f32(x2T[:, p.parity, 0, k, :]),
                                    ALU.subtract).then_inc(b_xTlo, 1)

            def top2(p):
                dve.wait_ge(b_lgt, p.count(1, 1))
                V.tensor_copy(lg[:], psM[:, 1, 0:TPP * E].rearrange("p (t e) -> p t e", t=TPP)).then_inc(b_lg, 1)
                dve.wait_ge(b_lg, p.count(1, 1))
                V.memset(gate[:, 2:3], 0.0)
                for t in range(TPP):
                    last = V.max(top[:, t, :], lg[:, t, :])
                last.then_inc(b_top, 1)
                dve.wait_ge(b_top, p.count(1, 1))
                V.memset(gate[:, 3:4], 0.0)
                for t in range(TPP):
                    last = V.max_index(topi[:, t, :], top[:, t, :], lg[:, t, :])
                last.then_inc(b_topi, 1)
                V.tensor_tensor(ex[:], lg[:], top[:, :, 0:1].broadcast_to([P, TPP, E]), ALU.subtract
                                ).then_inc(b_sub, 1)
                dve.wait_ge(b_topi, p.count(1, 1))
                V.tensor_copy(topf[:], topi[:]).then_inc(b_topf, 1)
                dve.wait_ge(b_topf, p.count(1, 1))
                for n in range(2):
                    last = V.tensor_tensor(hot[:, n], iota[:].unsqueeze(1).broadcast_to([P, TPP, E]),
                                           topf[:, :, n:n + 1].broadcast_to([P, TPP, E]), ALU.is_equal)
                last.then_inc(b_hot, 1)

            def coefs(p):
                dve.wait_ge(b_exp, p.count(1, 1))
                V.tensor_reduce(esum[:], ex[:], AX.X, ALU.add).then_inc(b_sum, 1)
                dve.wait_ge(b_hot, p.count(1, 1))
                V.tensor_tensor(hot[:, 0], hot[:, 0], hot[:, 1], ALU.add).then_inc(b_sel, 1)
                dve.wait_ge(b_sum, p.count(1, 1))
                V.reciprocal(einv[:], esum[:]).then_inc(b_inv, 1)
                dve.wait_ge(b_sel, p.count(2, 1))
                V.tensor_tensor(ex[:], ex[:], hot[:, 0], ALU.mult).then_inc(b_sel, 1)
                dve.wait_ge(b_inv, p.count(1, 1))
                dve.wait_ge(b_sel, p.count(2, 2))
                V.tensor_tensor(ex[:], ex[:], einv[:].unsqueeze(2).broadcast_to([P, TPP, E]), ALU.mult
                                ).then_inc(b_cf, 1)
                dve.wait_ge(b_cf, p.count(2, 1))
                V.tensor_scalar(coef[:, p.parity], ex[:], gains[:, 3:4], None, ALU.mult).then_inc(b_cf, 1)

            def hidden(p, m):
                c = m % 2
                dve.wait_ge(b_sil, p.count(NCH, m + 1))
                dve.wait_ge(b_u, p.count(NCH, m + 1))
                if p.has(NCH, m - 1):
                    dve.wait_ge(b_hlo, p.count(NCH, m - 1))
                V.tensor_tensor(hf[:, c, :], psS[:, 2 * c + 1, :], sil[c], ALU.mult).then_inc(b_h, 1)

            def hidden_lo(p, m):
                dve.wait_ge(b_hhi, p.count(NCH, m + 1))
                V.tensor_tensor(h2[:, m % 2, 1, :], hf[:, m % 2, :], f32(h2[:, m % 2, 0, :]), ALU.subtract
                                ).then_inc(b_hlo, 1)

            def add_up(p, m):
                if m == 0:
                    return
                dve.wait_ge(b_y, p.count(NCH, m + 1))
                if p.has(NCH - NSH + 1, m - 1):
                    dve.wait_ge(b_acc, p.count(NCH - NSH + 1, m - 1))
                if m == NSH - 1:
                    acc = x1p[:, p.parity].rearrange("p (a b) c -> p a (b c)", a=2)
                    last = V.scalar_tensor_tensor(acc, psT[:], gains[:, 3:4], acc, ALU.mult, ALU.add)
                else:
                    dve.wait_ge(b_cf, p.count(2, 2))
                    for t in range(TPP):
                        last = V.scalar_tensor_tensor(
                            x1p[:, p.parity, t, :], psT[:, t // 2, (t % 2) * D:(t % 2 + 1) * D],
                            coef[:, p.parity, t, m - NSH:m - NSH + 1], x1p[:, p.parity, t, :],
                            ALU.mult, ALU.add)
                last.then_inc(b_acc, 1)

            def pair(p, prep, nxt):
                for m in range(NCH):
                    ahead, nm = (p, m + 1) if m + 1 < NCH else (p.plus(1), 0)
                    if m + 1 < NCH or nxt:
                        hidden(ahead, nm)
                    if m > 0:
                        add_up(p, m - 1)
                    elif not isinstance(p.k, int) or p.off > 0:
                        add_up(p.plus(-1), NCH - 1)
                    if m + 1 < NCH or nxt:
                        hidden_lo(ahead, nm)
                    if prep and m == 2:
                        stats2(p.plus(1))
                    if prep and m == 3:
                        norm2(p.plus(1))
                    if prep and m == 4:
                        lo(p.plus(1))
                    if prep and m == 6:
                        top2(p.plus(1))
                    if prep and m == 8:
                        coefs(p.plus(1))

            stats2(Step(0, 0))
            norm2(Step(0, 0))
            lo(Step(0, 0))
            top2(Step(0, 0))
            coefs(Step(0, 0))
            hidden(Step(0, 0), 0)
            hidden_lo(Step(0, 0), 0)
            pair(Step(0, 0), True, True)
            with dve.Fori(0, (NPAIR - 2) // 2) as k:
                pair(Step(k, 1), True, True)
                pair(Step(k, 2), True, True)
            pair(Step(0, NPAIR - 1), False, False)
            add_up(Step(0, NPAIR - 1), NCH - 1)

        @block.gpsimd
        def _(pool):
            G = nc.gpsimd

            def inv_std(step, n, mv_done, eps_done, rstd_done):
                pool.wait_ge(mv_done, step.count(1, 1))
                G.tensor_tensor(rstd[:, 0:n], mv[:, 0:n, 1], eps[:, 0:n], ALU.add).then_inc(eps_done, 1)
                pool.wait_ge(eps_done, step.count(1, 1))
                G.tensor_tensor(rstd[:, 0:n], rstd[:, 0:n], half_neg[:, 0:n], ALU.pow).then_inc(rstd_done, 1)

            def normalise(i, t):
                pool.wait_ge(a_rden, i.count(2, t + 1))
                for g2 in range(0, NG, 2):
                    v = pr[:, i.parity, t, g2:g2 + 2].rearrange("p g (k j) -> p g k j", j=HPG)
                    last = G.tensor_tensor(v, v, rden[:, t, HPG * g2:HPG * (g2 + 2)].rearrange("p (g j) -> p g j", g=2
                                           ).unsqueeze(2).broadcast_to([P, 2, LK, HPG]), ALU.mult)
                last.then_inc(a_pn, 1)

            def bias(b):
                pool.wait_ge(a_res[b.parity], b.loads())
                if b.has(1, 0):
                    pool.wait_ge(a_x1, b.count(1, 0))
                G.tensor_tensor(xbias[:], xres[:, b.parity], bo_g[:].unsqueeze(1).broadcast_to([P, TPB, D]),
                                ALU.add).then_inc(a_xb, 1)

            def queries_lo(b):
                pool.wait_ge(a_qhi, b.count(1, 1))
                if b.has(4, 0):
                    pool.wait_ge(a_s, b.count(4, 0))
                for r in range(2):
                    rs, ro = slice(64 * r, 64 * r + 64), slice(64 * (1 - r), 64 * (1 - r) + 64)
                    G.tensor_tensor(qst[ro, r::2, :], qf[rs, :, :], f32(qst[rs, r::2, :]), ALU.subtract
                                    ).then_inc(a_qlo, 1)
                    pool.wait_ge(a_qlo, b.count(2, r + 1))

            def keys_spread_hi(b):
                pool.wait_ge(a_kthi, b.count(1, 1))
                if b.has(4, 0):
                    pool.wait_ge(a_s, b.count(4, 0))
                G.tensor_tensor(kbd[:, 0].rearrange("p g k j -> p (g k) j"),
                                f32(kt2[:, 0]).rearrange("p g k -> p (g k)").unsqueeze(2).broadcast_to([P, NG * LK, HPG]),
                                mask[:, 0].unsqueeze(1).broadcast_to([P, NG * LK, HPG]), ALU.mult
                                ).then_inc(a_kbhi, 1)

            def attended_lo(b):
                pool.wait_ge(a_ohi, b.count(1, 1))
                G.tensor_tensor(oT[:, 1], of[:], f32(oT[:, 0]), ALU.subtract).then_inc(a_olo, 1)

            def values_lo(b):
                pool.wait_ge(a_vhi, b.count(1, 1))
                G.tensor_tensor(vbd[:, :, 1, :], vm[:].rearrange("p a j d -> p a (j d)"), f32(vbd[:, :, 0, :]),
                                ALU.subtract).then_inc(a_vlo, 1)

            def iteration(i):
                if live(i, -1):
                    if live(i, -3):
                        pool.wait_ge(a_vlo, i.plus(-3).count(1, 1))
                    elif live(i, -4):
                        pool.wait_ge(a_xb, i.plus(-4).count(1, 1))
                    elif live(i):
                        pool.wait_ge(a_rstd, i.count(1, 1))
                    elif live(i, -2):
                        pool.wait_ge(a_kbhi, i.plus(-2).count(1, 1))
                    queries_lo(i.plus(-1))
                    keys_spread_hi(i.plus(-1))
                if live(i, -2):
                    normalise(i.plus(-2), 0)
                if live(i, 1):
                    inv_std(i.plus(1), TPB, a_mv, a_eps, a_rstd)
                if live(i, -3):
                    attended_lo(i.plus(-3))
                    bias(i.plus(-3))
                if live(i, -2):
                    normalise(i.plus(-2), 1)
                    values_lo(i.plus(-2))

            pool.wait_ge(w_zero, 3)
            pool.wait_ge(w_bias, 4)
            for i in range(FIRST, PEEL):
                iteration(Step(0, i))
            with pool.Fori(0, (B - 3 - PEEL) // 2) as k:
                iteration(Step(k, PEEL))
                iteration(Step(k, PEEL + 1))
            for i in range(B - 3, LAST + 1):
                iteration(Step(0, i))

            inv_std(Step(0, 0), TPP, b_mv, b_eps, b_rstd)
            inv_std(Step(0, 1), TPP, b_mv, b_eps, b_rstd)
            with pool.Fori(0, (NPAIR - 2) // 2) as k:
                inv_std(Step(k, 2), TPP, b_mv, b_eps, b_rstd)
                inv_std(Step(k, 3), TPP, b_mv, b_eps, b_rstd)




_INS = ['x', 'ctx_512', 'g_xattn', 'g_ffn', 'L0_xattn_Wq', 'L0_xattn_bq', 'L0_xattn_Wk', 'L0_xattn_bk',
        'L0_xattn_Wv', 'L0_xattn_bv', 'L0_xattn_Wo', 'L0_xattn_bo', 'L0_ffn_router', 'L0_ffn_experts_gate',
        'L0_ffn_experts_up', 'L0_ffn_experts_down', 'L0_ffn_shared_gate', 'L0_ffn_shared_up',
        'L0_ffn_shared_down']


def kernel(**inputs):
    import numpy as np
    import concourse.bacc as bacc
    from concourse.bass_utils import run_bass_kernel_spmd

    nc = bacc.Bacc("TRN2", target_bir_lowering=False, num_devices=1)
    arrays = {name: np.ascontiguousarray(inputs[name]) for name in _INS}
    arrays["ident"] = np.eye(P, dtype=np.float32)
    row = np.arange(P)[:, None]
    arrays["head_masks"] = np.stack([row % (HPG * DK) // DK == np.arange(HPG), row % HPG == np.arange(HPG)],
                                    1).astype(np.float32)
    arrays["expert_numbers"] = np.tile(np.arange(E, dtype=np.float32), (P, 1))
    args = [nc.dram_tensor("in_" + n, a.shape, mybir.dt.from_np(a.dtype), kind="ExternalInput").ap()
            for n, a in arrays.items()]
    out = nc.dram_tensor("out", (B * S, D), F32, kind="ExternalOutput").ap()
    build(nc, *args, out)
    r = run_bass_kernel_spmd(nc, [{"in_" + n: a for n, a in arrays.items()}], core_ids=[0])
    return r.results[0]["out"].reshape(B, S, D)
```
